# Optimizing a Trainium2 kernel written in Bass

```python
import numpy as np
import jax
import jax.numpy as jnp

def _softmax(x, axis=-1):
    return jax.nn.softmax(x, axis=axis)

def _gelu(x):
    return jax.nn.gelu(x, approximate=True)

def _silu(x):
    return jax.nn.silu(x)

def _sigmoid(x):
    return jax.nn.sigmoid(x)

def _layernorm(x, axis=-1, eps=1e-05):
    m = jnp.mean(x, axis=axis, keepdims=True)
    v = jnp.var(x, axis=axis, keepdims=True)
    return (x - m) / jnp.sqrt(v + eps)

def _scatter_add(tgt, idx, src, axis=0):
    return tgt.at[idx].add(src)

def _segment_sum(src, seg, n):
    return jax.ops.segment_sum(src, seg, n)
kernel_name = 'mk_flamingo_gated_d1_seqx_r8_df9345'

def setup_inputs(seed: int=0):
    np.random.seed(seed)
    _w = jnp.asarray

    def _rec_inputs():
        import jax
        import jax.numpy as jnp
        _rk = jax.random.key(seed)
        x = -0.0002928 + 1 * jax.random.normal(jax.random.fold_in(_rk, 1), (8, 256, 128), jnp.float32)
        _lenS = 256 - jax.random.randint(jax.random.fold_in(_rk, 7), (8,), 0, max(1, 256 // 4) + 1, jnp.int32)
        _lenS2 = 256 - jax.random.randint(jax.random.fold_in(_rk, 8), (8,), 0, max(1, 256 // 4) + 1, jnp.int32)
        _ctx_1024P = jax.random.normal(jax.random.fold_in(_rk, 11), (8, 16, 128), jnp.float32)
        _ctx_1024c = jax.random.dirichlet(jax.random.fold_in(_rk, 511), 0.3 * jnp.ones((16,), jnp.float32), (8, 256))
        _ctx_1024t = jnp.einsum('bsk,bkd->bsd', _ctx_1024c, _ctx_1024P)
        _ctx_1024t = _ctx_1024t * jax.lax.rsqrt(jnp.mean(jnp.square(_ctx_1024t)) + 1e-12) * 0.953939
        ctx_1024 = -1.39393e-06 + 0.999914 * (_ctx_1024t + 0.3 * jax.random.normal(jax.random.fold_in(_rk, 611), (8, 256, 128), jnp.float32))
        _g = jax.random.normal(jax.random.fold_in(_rk, 9001), (2, 1), jnp.float32)
        _g = jnp.sign(_g) * jnp.maximum(jnp.abs(_g), 1.0) + (_g == 0) * 1.0
        g_xattn = _g[0]
        g_ffn = _g[1]
        return (x, ctx_1024, g_xattn, g_ffn)
    x, ctx_1024, g_xattn, g_ffn = _rec_inputs()

    def _L0_xattn_setup():
        import jax, jax.numpy as jnp
        import numpy as np
        import math
        D_MODEL = 128
        NUM_HEADS = 16
        MAX_LEN = 256
        D_HEAD = D_MODEL // NUM_HEADS
        BATCH = 2
        SEQ = 256

        def _skew(QEr):
            B, H, R, C = QEr.shape
            padded = jnp.pad(QEr, ((0, 0), (0, 0), (0, 0), (1, 0)))
            reshaped = padded.reshape(B, H, C + 1, R)
            return reshaped[:, :, 1:, :]
        root = jax.random.key(seed)
        ks = jax.random.split(root, 10)
        s = 1.0 / math.sqrt(D_MODEL)
        return {'query': jax.random.normal(ks[0], (BATCH, SEQ, D_MODEL), jnp.float32), 'key': jax.random.normal(ks[1], (BATCH, SEQ, D_MODEL), jnp.float32), 'value': jax.random.normal(ks[2], (BATCH, SEQ, D_MODEL), jnp.float32), 'Wq': jax.random.normal(ks[3], (D_MODEL, D_MODEL), jnp.float32) * s, 'bq': jax.random.normal(ks[4], (D_MODEL,), jnp.float32) * s, 'Wk': jax.random.normal(ks[5], (D_MODEL, D_MODEL), jnp.float32) * s, 'bk': jax.random.normal(ks[6], (D_MODEL,), jnp.float32) * s, 'Wv': jax.random.normal(ks[7], (D_MODEL, D_MODEL), jnp.float32) * s, 'bv': jax.random.normal(ks[8], (D_MODEL,), jnp.float32) * s, 'Er': jax.random.normal(ks[9], (MAX_LEN, D_HEAD), jnp.float32)}
    _L0_xattn_all = _L0_xattn_setup()
    _L0_xattn_in = {k: v for k, v in _L0_xattn_all.items() if k in ('Wq', 'bq', 'Wk', 'bk', 'Wv', 'bv', 'Er')}
    del _L0_xattn_all

    def _L0_ffn_setup():
        import jax, jax.numpy as jnp
        import numpy as np
        S, B, D = (128, 2, 128)
        E, TOPK = (15, 3)
        F = 128
        FS = 256

        def _uinit(k, shape, out_dim):
            std = out_dim ** (-0.5)
            return jax.random.uniform(k, shape, jnp.float32, -std, std)
        key = jax.random.key(seed)
        ks = jax.random.split(key, 10)
        return {'x': jax.random.normal(ks[0], (S, B, D), jnp.float32), 'gate_w': jax.random.normal(ks[1], (E, D), jnp.float32) * D ** (-0.5), 'fc1_w': _uinit(ks[2], (E, 2 * F, D), 2 * F), 'fc1_b': _uinit(ks[3], (E, 2 * F), 2 * F), 'geglu_mult': jnp.ones((E, F), jnp.float32), 'fc2_w': _uinit(ks[4], (E, D, F), D), 'fc2_b': _uinit(ks[5], (E, D), D), 's_fc1_w': _uinit(ks[6], (2 * FS, D), 2 * FS), 's_fc1_b': _uinit(ks[7], (2 * FS,), 2 * FS), 's_geglu_mult': jnp.ones((FS,), jnp.float32), 's_fc2_w': _uinit(ks[8], (D, FS), D), 's_fc2_b': _uinit(ks[9], (D,), D)}
    _L0_ffn_all = _L0_ffn_setup()
    _L0_ffn_in = {k: v for k, v in _L0_ffn_all.items() if k in ('gate_w', 'fc1_w', 'fc1_b', 'geglu_mult', 'fc2_w', 'fc2_b', 's_fc1_w', 's_fc1_b', 's_geglu_mult', 's_fc2_w', 's_fc2_b')}
    del _L0_ffn_all
    return {'x': x, 'ctx_1024': ctx_1024, 'g_xattn': g_xattn, 'g_ffn': g_ffn, 'L0_xattn_Wq': _L0_xattn_in['Wq'], 'L0_xattn_bq': _L0_xattn_in['bq'], 'L0_xattn_Wk': _L0_xattn_in['Wk'], 'L0_xattn_bk': _L0_xattn_in['bk'], 'L0_xattn_Wv': _L0_xattn_in['Wv'], 'L0_xattn_bv': _L0_xattn_in['bv'], 'L0_xattn_Er': _L0_xattn_in['Er'], 'L0_ffn_gate_w': _L0_ffn_in['gate_w'], 'L0_ffn_fc1_w': _L0_ffn_in['fc1_w'], 'L0_ffn_fc1_b': _L0_ffn_in['fc1_b'], 'L0_ffn_geglu_mult': _L0_ffn_in['geglu_mult'], 'L0_ffn_fc2_w': _L0_ffn_in['fc2_w'], 'L0_ffn_fc2_b': _L0_ffn_in['fc2_b'], 'L0_ffn_s_fc1_w': _L0_ffn_in['s_fc1_w'], 'L0_ffn_s_fc1_b': _L0_ffn_in['s_fc1_b'], 'L0_ffn_s_geglu_mult': _L0_ffn_in['s_geglu_mult'], 'L0_ffn_s_fc2_w': _L0_ffn_in['s_fc2_w'], 'L0_ffn_s_fc2_b': _L0_ffn_in['s_fc2_b']}

def reference(x, ctx_1024, g_xattn, g_ffn, L0_xattn_Wq, L0_xattn_bq, L0_xattn_Wk, L0_xattn_bk, L0_xattn_Wv, L0_xattn_bv, L0_xattn_Er, L0_ffn_gate_w, L0_ffn_fc1_w, L0_ffn_fc1_b, L0_ffn_geglu_mult, L0_ffn_fc2_w, L0_ffn_fc2_b, L0_ffn_s_fc1_w, L0_ffn_s_fc1_b, L0_ffn_s_geglu_mult, L0_ffn_s_fc2_w, L0_ffn_s_fc2_b):
    import jax
    import jax.numpy as jnp

    def _L0_xattn_ref(query, key, value, Wq, bq, Wk, bk, Wv, bv, Er):
        import jax, jax.numpy as jnp
        import numpy as np
        import math
        D_MODEL = 128
        NUM_HEADS = 16
        MAX_LEN = 256
        D_HEAD = D_MODEL // NUM_HEADS
        BATCH = 2
        SEQ = 256

        def _skew(QEr):
            B, H, R, C = QEr.shape
            padded = jnp.pad(QEr, ((0, 0), (0, 0), (0, 0), (1, 0)))
            reshaped = padded.reshape(B, H, C + 1, R)
            return reshaped[:, :, 1:, :]
        B, S, D = query.shape
        H, dh = (NUM_HEADS, D_HEAD)
        q = (jnp.einsum('bsd,ed->bse', query, Wq) + bq).reshape(B, S, H, dh).transpose(0, 2, 1, 3)
        k = (jnp.einsum('bsd,ed->bse', key, Wk) + bk).reshape(B, S, H, dh).transpose(0, 2, 1, 3)
        v = (jnp.einsum('bsd,ed->bse', value, Wv) + bv).reshape(B, S, H, dh).transpose(0, 2, 1, 3)
        start = MAX_LEN - S
        Er_s = Er[start:, :]
        QEr = jnp.einsum('bhsd,ld->bhsl', q, Er_s)
        Srel = _skew(QEr)
        QK = jnp.einsum('bhsd,bhtd->bhst', q, k)
        attn = (QK + Srel) / math.sqrt(dh)
        causal = jnp.tril(jnp.ones((S, S), dtype=bool))
        attn = jnp.where(causal[None, None], attn, -jnp.inf)
        attn = jax.nn.softmax(attn, axis=-1)
        out = jnp.einsum('bhst,bhtd->bhsd', attn, v)
        out = out.transpose(0, 2, 1, 3).reshape(B, S, D)
        return out

    def _L0_ffn_ref(x, gate_w, fc1_w, fc1_b, geglu_mult, fc2_w, fc2_b, s_fc1_w, s_fc1_b, s_geglu_mult, s_fc2_w, s_fc2_b):
        import jax, jax.numpy as jnp
        import numpy as np
        S, B, D = (128, 2, 128)
        E, TOPK = (15, 3)
        F = 128
        FS = 256

        def _uinit(k, shape, out_dim):
            std = out_dim ** (-0.5)
            return jax.random.uniform(k, shape, jnp.float32, -std, std)
        s, b, d = x.shape
        xt = x.reshape(-1, d)
        T = xt.shape[0]
        logits = xt @ gate_w.T
        scores = jax.nn.softmax(logits, axis=-1)
        topk_w, topk_idx = jax.lax.top_k(scores, TOPK)
        topk_w = topk_w / (jnp.sum(topk_w, axis=-1, keepdims=True) + 1e-20)
        comb = jnp.zeros((T, E), xt.dtype).at[jnp.arange(T)[:, None], topk_idx].add(topk_w)
        h = jnp.einsum('td,efd->etf', xt, fc1_w) + fc1_b[:, None, :]
        xh, g = (h[..., :F], h[..., F:])
        a = jax.nn.gelu(g, approximate=False) * xh * geglu_mult[:, None, :]
        yexp = jnp.einsum('etf,edf->etd', a, fc2_w) + fc2_b[:, None, :]
        y = jnp.einsum('etd,te->td', yexp, comb)
        hs = xt @ s_fc1_w.T + s_fc1_b
        xs, gs = (hs[..., :FS], hs[..., FS:])
        as_ = jax.nn.gelu(gs, approximate=False) * xs * s_geglu_mult
        ys = as_ @ s_fc2_w.T + s_fc2_b
        return (y + ys).reshape(s, b, d)
    x = x + jnp.tanh(g_xattn[0]) * _L0_xattn_ref(_layernorm(x, axis=-1), ctx_1024, ctx_1024, L0_xattn_Wq, L0_xattn_bq, L0_xattn_Wk, L0_xattn_bk, L0_xattn_Wv, L0_xattn_bv, L0_xattn_Er)
    x = x + jnp.tanh(g_ffn[0]) * _L0_ffn_ref(_layernorm(x, axis=-1), L0_ffn_gate_w, L0_ffn_fc1_w, L0_ffn_fc1_b, L0_ffn_geglu_mult, L0_ffn_fc2_w, L0_ffn_fc2_b, L0_ffn_s_fc1_w, L0_ffn_s_fc1_b, L0_ffn_s_geglu_mult, L0_ffn_s_fc2_w, L0_ffn_s_fc2_b)
    return x

_drawn_inputs = setup_inputs


def setup_inputs(seed=0):
    import zlib

    import numpy as np

    out = dict(_drawn_inputs(seed))
    spreads = {'L0_ffn_geglu_mult': (1.0, 0.6), 'L0_ffn_s_geglu_mult': (1.0, 0.6)}
    factors = {'L0_xattn_bq': 2.725, 'L0_xattn_bk': 8.0, 'L0_ffn_fc1_b': 8.0, 'L0_ffn_s_fc1_b': 8.0}
    for name, (base, spread) in spreads.items():
        noise = np.random.default_rng([zlib.crc32(name.encode()), seed]).standard_normal(out[name].shape)
        drawn = base * np.exp(spread * noise) if base else spread * noise
        out[name] = jnp.asarray(drawn.astype(out[name].dtype))
    for name, factor in factors.items():
        out[name] = (out[name] * factor).astype(out[name].dtype)
    return out
```

```python
from contextlib import ExitStack

import concourse.bass as bass
from concourse import mybir

F32 = mybir.dt.float32
BF16 = mybir.dt.bfloat16
ALU = mybir.AluOpType
ACT = mybir.ActivationFunctionType
AX = mybir.AxisListType

B, S, D = 8, 256, 128
H, DH = 16, 8
QB = 16
HG = 128 // QB
G = H // HG
J = S // (2 * QB)
TT = S // 128
E, TOPK = 15, 3
EX = E + 2
EC = E + 1
PAIRS = B // 2
PT_ = 2 * S
UW = S - 1 + 2 * QB
PADS = 8 - TOPK
PAD_VALUE = 2.0
EPS = 1e-5
TOP_EPS = 1e-20
MASKED = -1e30

ATTENTION = [
    "S00", "ln1a", "S01", "ln2b", "S02", "S03", "tr2", "U00", "ln1b", "S04", "gate", "S05", "tr1", "U01",
    "S06", "q", "S07", "route", "U02", "k", "U03", "S10", "v", "S11", "U04", "U05", "S12", "S13", "PV0",
    "U10", "comb", "S14", "S15", "U11", "S16", "S17", "U12", "U13", "U14", "U15", "PV1", "ln2a",
]
UNITS = [(0, 0, 0, 1), (0, 0, 4, 3), (1, 0, 8, 5), (2, 1, 8, 5), (1, 0, 12, 7), (2, 1, 12, 7)]
SLOTS = [(0, 0, 0), (1, 1, 0), (2, 1, 1)]


def flamingo_block(nc, x, ctxT, g_xattn, g_ffn, wqT, bq, wkT, bk, wvT, bv, erw, gateT,
                   w1T, b1x, b1g, mult, w2T, b2, identity, head_mask, query_mask, causal, onehot, out):
    with ExitStack() as ctx:
        def sb(name, shape, dt=F32):
            return ctx.enter_context(nc.sbuf_tensor(name, shape, dt))

        def sem(name):
            return ctx.enter_context(nc.semaphore(name))

        wq_s, wk_s, wv_s = sb("wq_s", [D, D]), sb("wk_s", [D, D]), sb("wv_s", [D, D])
        bq_s, bk_s = sb("bq_s", [D, 1]), sb("bk_s", [D, 1])
        bq_scaled = sb("bq_scaled", [D, 1])
        bv_s = sb("bv_s", [128, D])
        erw_s = sb("erw_s", [QB * DH, UW])
        gate_s = sb("gate_s", [D, E])
        w1_s, w2_s = sb("w1_s", [D, EX, 256]), sb("w2_s", [128, EX, D])
        b1x_s, b1g_s, mult_s = sb("b1x_s", [128, EX]), sb("b1g_s", [128, EX]), sb("mult_s", [128, EX])
        b2_s = sb("b2_s", [EC, D])
        id_s, idb_s = sb("id_s", [128, 128]), sb("idb_s", [128, 128], BF16)
        hm_s, qm_s = sb("hm_s", [128, HG]), sb("qm_s", [128, QB])
        causal_f, causal_s = sb("causal_f", [2 * QB, 2, 128]), sb("causal_s", [2 * QB, 2, 128], BF16)
        oh_f, oh_s = sb("oh_f", [3 * EC, E, 128]), sb("oh_s", [3 * EC, E, 128], BF16)
        g_s, tanh_s = sb("g_s", [128, 2]), sb("tanh_s", [128, 2])
        half_s = sb("half_s", [128, TT])
        x_s = sb("x_s", [128, B, S])
        stats, mv, var, rstd = (sb("stats", [128, TT, 6]), sb("mv", [128, TT, 2]), sb("var", [128, TT]),
                                sb("rstd", [128, TT]))
        stats2, mv2, var2, rstd2 = (sb("stats2", [128, TT, 6]), sb("mv2", [128, TT, 2]), sb("var2", [128, TT]),
                                    sb("rstd2", [128, TT]))
        xn, xn2 = sb("xn", [128, S]), sb("xn2", [128, S])
        xnT = sb("xnT", [D, S])
        c_s = sb("c_s", [D, 2, S])
        qT, kT = sb("qT", [D, 2, S]), sb("kT", [D, 2, S])
        NB = S // QB
        q_over_heads = sb("q_over_heads", [D, 2, NB, HG, QB])
        q_spread_s = sb("q_spread_s", [QB * DH, H, S])
        q_over_queries = sb("q_over_queries", [QB * DH, 2, NB, H, QB])
        v_s = sb("v_s", [128, 2, TT, H, DH + 1])
        negmax = sb("negmax", [128, G, J, 2])
        p_s = sb("p_s", [128, G, 2 * J, S])
        pt_s = sb("pt_s", [128, G, 3, HG, 128])
        rden, attn = sb("rden", [128, TT * H]), sb("attn", [128, TT * H, DH])
        x2T = sb("x2T", [D, PT_])
        ngate, logit, prob = sb("ngate", [128, TT]), sb("logit", [128, TT, E]), sb("prob", [128, TT, E])
        psum_, top, rest = sb("psum_", [128, TT]), sb("top", [128, TT, 8]), sb("rest", [128, TT, E + PADS])
        padded = sb("padded", [128, TT, E + PADS])
        comb, comb_r, comb3 = (sb("comb", [128, TT, EC]), sb("comb_r", [128, TT, EC]),
                               sb("comb3", [128, TT, 3 * EC], BF16))
        combT, comb3T = sb("combT", [EC, PT_]), sb("comb3T", [3 * EC, PT_], BF16)
        gelu_s, act1, act2 = sb("gelu_s", [128, 2, PT_]), sb("act1", [128, 2, PT_]), sb("act2", [128, 2, PT_])
        yT, out_s = sb("yT", [D, PT_]), sb("out_s", [128, PT_])
        q_dram = nc.dram_tensor("q_scratch", (2, D, S), F32, kind="Internal").ap()

        sc = [ctx.enter_context(nc.psum_tensor(f"sc{i}", [128, 512], F32)) for i in range(4)]
        tp = [ctx.enter_context(nc.psum_tensor(f"tp{i}", [128, 512], F32)) for i in range(2)]
        acc = ctx.enter_context(nc.psum_tensor("acc", [128, 512], F32))
        misc = ctx.enter_context(nc.psum_tensor("misc", [128, 512], F32))
        pv_v = acc[:, 0:TT * H * (DH + 1)].rearrange("p (t h d) -> p t h d", t=TT, h=H)

        attn_loaded, x_loaded, moe_loaded = sem("attn_loaded"), sem("x_loaded"), sem("moe_loaded")
        ctx_loaded = [sem(f"ctx_loaded{p}") for p in range(2)]
        q_stored = [sem(f"q_stored{p}") for p in range(2)]
        q_spread = [sem(f"q_spread{p}") for p in range(2)]
        spread_free = sem("spread_free")
        out_stored, out_free = sem("out_stored"), sem("out_free")
        consts_ready, scaled_bias, tanh_ready, w2_scaled, half_ready = (
            sem("consts_ready"), sem("scaled_bias"), sem("tanh_ready"), sem("w2_scaled"), sem("half_ready"))
        var1_ready, rstd1_ready, xn1_ready = sem("var1_ready"), sem("rstd1_ready"), sem("xn1_ready")
        tr1_done, xnT_ready = sem("tr1_done"), sem("xnT_ready")
        q_done, q_ready, k_done, k_ready, v_done, v_ready = (
            sem("q_done"), sem("q_ready"), sem("k_done"), sem("k_ready"), sem("v_done"), sem("v_ready"))
        heads_ready, queries_ready = sem("heads_ready"), sem("queries_ready")
        scores_done, max_ready, exp_ready = sem("scores_done"), sem("max_ready"), sem("exp_ready")
        pt_done = sem("pt_done")
        pt_ready = [sem("pt_ready_act"), sem("pt_ready_dve")]
        pv_done, pv_read, x1_ready = sem("pv_done"), sem("pv_read"), sem("x1_ready")
        var2_ready, rstd2_ready, xn2_ready = sem("var2_ready"), sem("rstd2_ready"), sem("xn2_ready")
        tr2_done, x2T_ready, gate_done, gate_read, logits_ready, probs_ready = (
            sem("tr2_done"), sem("x2T_ready"), sem("gate_done"), sem("gate_read"), sem("logits_ready"),
            sem("probs_ready"))
        comb_ready, combT_done, combT_ready = sem("comb_ready"), sem("combT_done"), sem("combT_ready")
        gate_half_done, up_half_done, gelu_ready, act_ready, y_done, yT_ready, yback_done, out_ready = (
            sem("gate_half_done"), sem("up_half_done"), sem("gelu_ready"), sem("act_ready"), sem("y_done"),
            sem("yT_ready"), sem("yback_done"), sem("out_ready"))
        block = ctx.enter_context(nc.Block())

        N_ATTN, N_MOE = 11, 8
        x_view = x.rearrange("b (t p) d -> p b t d", p=128)
        out_view = out.rearrange("b (t p) d -> p b t d", p=128)

        def copy_pt(eng, copy, b, g, u):
            eng.wait_ge(pt_done, len(UNITS) * (G * b + g) + u + 1)
            slot, _, blk, _ = UNITS[u]
            q0 = blk % 8 * QB
            dst = pt_s[:, g, slot, :, q0:q0 + 4 * QB].rearrange("p h (k i) -> p h k i", k=4)
            src = tp[u % 2][:, :].rearrange("p (k h i) -> p h k i", k=4, h=HG)
            copy(dst, src).then_inc(pt_ready[u % 2], 1)

        @block.sync
        def _(sp):
            def load_ctx(at, p):
                sp.dma_start(c_s[:, p, :], ctxT[:, bass.ds(at, S)]).then_inc(ctx_loaded[p], 16)

            sp.sem_inc(out_free, 1)
            for dst, src in ((id_s, identity), (wq_s, wqT), (bq_s, bq)):
                sp.dma_start(dst[:, :], src).then_inc(attn_loaded, 16)
            for b in range(B):
                sp.dma_start(x_s[:, b, :].rearrange("p (t d) -> p t d", t=TT), x_view[:, b]).then_inc(x_loaded, 16)
                if b == 0:
                    load_ctx(0, 0)
                    load_ctx(S, 1)
            for dst, src in ((wk_s, wkT), (bk_s, bk), (wv_s, wvT), (erw_s, erw), (hm_s, head_mask),
                             (qm_s, query_mask)):
                sp.dma_start(dst[:, :], src).then_inc(attn_loaded, 16)
            sp.dma_start(causal_f[:, :, :], causal).then_inc(attn_loaded, 16)
            sp.dma_start(bv_s[:, :], bv.partition_broadcast(128)).then_inc(attn_loaded, 16)

            def spread_q(b, p, k):
                sp.wait_ge(q_ready, b + 1)
                sp.wait_ge(spread_free, b + 1)
                sp.dma_start(q_dram[p], qT[:, p, :]).then_inc(q_stored[p], 16)
                sp.wait_ge(q_stored[p], 16 * (k + 1))
                src = q_dram[p].rearrange("(h d) s -> d h s", d=DH)
                for i in range(QB):
                    sp.dma_start(q_spread_s[i * DH:(i + 1) * DH, :, :], src).then_inc(q_spread[p], 16)

            for dst, src in ((gate_s, gateT), (b1x_s, b1x), (b1g_s, b1g), (mult_s, mult), (b2_s, b2)):
                sp.dma_start(dst[:, :], src).then_inc(moe_loaded, 16)
            for dst, src in ((w1_s, w1T), (w2_s, w2T), (oh_f, onehot)):
                sp.dma_start(dst[:, :, :], src).then_inc(moe_loaded, 16)
            spread_q(0, 0, 0)

            spread_q(1, 1, 0)
            with sp.Fori(0, PAIRS - 1) as i:
                even, odd, pair = sp.snap((2 * i + 2) * S), sp.snap((2 * i + 3) * S), sp.snap(2 * i)
                sp.wait_ge(v_ready, 2 * i + 1)
                load_ctx(even, 0)
                spread_q(2 * i + 2, 0, i + 1)
                sp.wait_ge(v_ready, 2 * i + 2)
                load_ctx(odd, 1)
                spread_q(2 * i + 3, 1, i + 1)
                sp.wait_ge(out_ready, i + 2)
                sp.dma_start(out_view[:, bass.ds(pair, 2)],
                             out_s[:, :].rearrange("p (b t d) -> p b t d", b=2, t=TT)).then_inc(out_stored, 16)
                sp.wait_ge(out_stored, 16 * (i + 1))
                sp.sem_inc(out_free, 1)
            sp.wait_ge(out_ready, PAIRS + 1)
            sp.dma_start(out_view[:, B - 2:B],
                         out_s[:, :].rearrange("p (b t d) -> p b t d", b=2, t=TT)).then_inc(out_stored, 16)
            sp.wait_ge(out_stored, 16 * PAIRS)

        @block.gpsimd
        def _(pool):
            nc.gpsimd.memset(half_s[:, :], -0.5).then_inc(half_ready, 1)
            pool.wait_ge(half_ready, 1)

            def rsqrt1(b):
                pool.wait_ge(var1_ready, b + 1)
                nc.gpsimd.tensor_tensor(rstd[:, :], var[:, :], half_s[:, :], ALU.pow).then_inc(rstd1_ready, 1)

            def rsqrt2(b):
                pool.wait_ge(var2_ready, b + 1)
                nc.gpsimd.tensor_tensor(rstd2[:, :], var2[:, :], half_s[:, :], ALU.pow).then_inc(rstd2_ready, 1)

            def mask_queries(b, p, k):
                pool.wait_ge(q_spread[p], 16 * QB * (k + 1))
                for c in range(4):
                    heads = slice(4 * c, 4 * c + 4)
                    nc.gpsimd.tensor_tensor(
                        q_over_queries[:, p, :, heads, :].rearrange("p k h i -> p h k i"),
                        q_spread_s[:, heads, :].rearrange("p h (k i) -> p h k i", i=QB),
                        qm_s[:, 0:QB].unsqueeze(1).unsqueeze(1).broadcast_to((128, 4, NB, QB)),
                        ALU.mult).then_inc(queries_ready, 1)
                pool.wait_ge(queries_ready, 4 * (b + 1))
                pool.sem_inc(spread_free, 1)

            pool.sem_inc(spread_free, 1)
            rsqrt1(0)
            pool.wait_ge(attn_loaded, 16 * N_ATTN)
            mask_queries(0, 0, 0)
            rsqrt1(1)
            mask_queries(1, 1, 0)
            with pool.Fori(0, PAIRS - 1) as i:
                for b, p, k in ((2 * i + 1, 1, i), (2 * i + 2, 0, i + 1)):
                    rsqrt2(b - 1)
                    rsqrt1(b + 1)
                    mask_queries(b + 1, 1 - p, i + 1)
            rsqrt2(B - 2)
            rsqrt2(B - 1)

        @block.scalar
        def _(act):
            act.wait_ge(attn_loaded, 16 * N_ATTN)
            act.dma_start(g_s[:, 0:1], g_xattn.partition_broadcast(128)).then_inc(tanh_ready, 16)
            act.dma_start(g_s[:, 1:2], g_ffn.partition_broadcast(128)).then_inc(tanh_ready, 16)
            act.wait_ge(tanh_ready, 32)
            nc.scalar.activation(tanh_s[:, :], g_s[:, :], ACT.Tanh).then_inc(tanh_ready, 1)
            act.sem_inc(combT_ready, 1)
            act.sem_inc(yT_ready, 1)
            nc.scalar.mul(bq_scaled[:, :], bq_s[:, :], DH ** -0.5).then_inc(scaled_bias, 1)
            act.wait_ge(scaled_bias, 1)

            def front_evac(step, b, p):
                if step == "tr1":
                    act.wait_ge(tr1_done, b + 1)
                    nc.scalar.copy(xnT[:, :], misc[:, 0:S]).then_inc(xnT_ready, 1)
                if step == "q":
                    act.wait_ge(q_done, b + 1)
                    nc.scalar.activation(qT[:, p, :], misc[:, 0:S], ACT.Identity, bias=bq_scaled[:, 0:1],
                                         scale=DH ** -0.5).then_inc(q_ready, 1)
                if step == "k":
                    act.wait_ge(k_done, b + 1)
                    nc.scalar.activation(kT[:, p, :], misc[:, 0:S], ACT.Identity,
                                         bias=bk_s[:, 0:1]).then_inc(k_ready, 1)

            def attention(b, p, front, tail):
                for step in ATTENTION:
                    if front:
                        front_evac(step, b + 1, 1 - p)
                    if tail and step == "tr2":
                        act.wait_ge(tr2_done, b)
                        nc.scalar.copy(x2T[:, (1 - p) * S:(2 - p) * S], misc[:, 0:S]).then_inc(x2T_ready, 1)
                    if tail and step == "route":
                        act.wait_ge(logits_ready, b)
                        nc.scalar.activation(prob[:, :, :], logit[:, :, :], ACT.Exp).then_inc(probs_ready, 1)
                    if tail and step == "comb":
                        copy_comb(b - 1, 1 - p)
                    if step[0] == "S":
                        g, j = int(step[1]), int(step[2])
                        act.wait_ge(max_ready, G * J * b + J * g + j + 1)
                        L = 2 * QB * (j + 1)
                        for c in range(2):
                            ins = nc.scalar.activation(p_s[:, g, 2 * j + c, 0:L], sc[j % 4][:, c * S:c * S + L],
                                                       ACT.Exp, bias=negmax[:, g, j, c:c + 1])
                        ins.then_inc(exp_ready, 1)
                    if step[0] == "U" and int(step[2]) % 2 == 0:
                        copy_pt(act, nc.scalar.copy, b, int(step[1]), int(step[2]))

            def copy_comb(b, p):
                act.wait_ge(combT_done, b + 1)
                nc.scalar.copy(comb3T[:, p * S:(p + 1) * S], misc[0:3 * EC, 0:S // 2].bitcast(BF16))
                nc.scalar.copy(combT[:, p * S:(p + 1) * S], misc[0:EC, S:2 * S]).then_inc(combT_ready, 1)

            def experts(i):
                for e in range(EX):
                    act.wait_ge(gate_half_done, EX * i + e + 1)
                    nc.scalar.activation(gelu_s[:, e % 2, :], sc[2 * (e % 2) + 1][:, :], ACT.Gelu,
                                         bias=b1g_s[:, e:e + 1]).then_inc(gelu_ready, 1)
                act.wait_ge(y_done, i + 1)
                nc.scalar.activation(yT[:, :], acc[:, :], ACT.Identity, scale=tanh_s[:, 1:2]).then_inc(yT_ready, 1)

            for step in ("tr1", "q", "k"):
                front_evac(step, 0, 0)
            attention(0, 0, True, False)
            act.wait_ge(moe_loaded, 16 * N_MOE)
            with act.Fori(0, PAIRS - 1) as i:
                attention(2 * i + 1, 1, True, True)
                attention(2 * i + 2, 0, True, True)
                experts(i)
            attention(B - 1, 1, False, True)
            act.wait_ge(tr2_done, B)
            nc.scalar.copy(x2T[:, S:2 * S], misc[:, 0:S]).then_inc(x2T_ready, 1)
            act.wait_ge(logits_ready, B)
            nc.scalar.activation(prob[:, :, :], logit[:, :, :], ACT.Exp).then_inc(probs_ready, 1)
            copy_comb(B - 1, 1)
            experts(PAIRS - 1)

        @block.vector
        def _(dve):
            def own(ins):
                dve.drain()

            dve.sem_inc(act_ready, 1)
            dve.sem_inc(out_ready, 1)
            nc.vector.memset(p_s[:, :, :, :], 0.0)
            nc.vector.memset(v_s[:, :, :, :, DH:DH + 1], 1.0)
            nc.vector.memset(padded[:, :, E:], PAD_VALUE)
            own(nc.vector.memset(comb[:, :, E:], 1.0))

            def stats_of(b, st, m, v, ready):
                for t in range(TT):
                    ins = nc.vector.bn_stats(st[:, t, :], x_s[:, bass.ds(b, 1), t * 128:(t + 1) * 128])
                own(ins)
                for t in range(TT):
                    ins = nc.vector.bn_aggr(m[:, t, :], st[:, t, :])
                own(ins)
                nc.vector.tensor_scalar(v[:, :], m[:, :, 1], EPS, None, ALU.add).then_inc(ready, 1)

            def normalise(b, m, r, dst, ready):
                for t in range(TT):
                    ins = nc.vector.tensor_scalar(dst[:, t * 128:(t + 1) * 128],
                                                  x_s[:, bass.ds(b, 1), t * 128:(t + 1) * 128],
                                                  m[:, t, 0:1], r[:, t:t + 1], ALU.subtract, ALU.mult)
                ins.then_inc(ready, 1)

            def front_work(step, b, p):
                if step == "ln1a":
                    stats_of(b, stats, mv, var, var1_ready)
                if step == "ln1b":
                    dve.wait_ge(rstd1_ready, b + 1)
                    normalise(b, mv, rstd, xn, xn1_ready)
                if step == "q":
                    dve.wait_ge(q_ready, b + 1)
                    nc.vector.tensor_tensor(
                        q_over_heads[:, p, :, :, :],
                        qT[:, p, :].rearrange("p (k i) -> p k i", i=QB).unsqueeze(2).broadcast_to((D, NB, HG, QB)),
                        hm_s[:, :].unsqueeze(1).unsqueeze(3).broadcast_to((D, NB, HG, QB)),
                        ALU.mult).then_inc(heads_ready, 1)
                if step == "v":
                    dve.wait_ge(v_done, b + 1)
                    nc.vector.tensor_tensor(
                        v_s[:, p, :, :, 0:DH],
                        misc[:, 0:S].rearrange("p (t h d) -> p t h d", t=TT, h=H),
                        bv_s[:, :].rearrange("p (h d) -> p h d", h=H).unsqueeze(1).broadcast_to((128, TT, H, DH)),
                        ALU.add).then_inc(v_ready, 1)

            def tail_work(step, b, p):
                if step == "ln2b":
                    dve.wait_ge(rstd2_ready, b + 1)
                    normalise(b, mv2, rstd2, xn2, xn2_ready)
                if step == "gate":
                    dve.wait_ge(gate_done, b + 1)
                    lg = misc[:, 0:TT * EC].rearrange("p (t e) -> p t e", t=TT)[:, :, 0:E]
                    own(nc.vector.tensor_reduce(ngate[:, :], lg, AX.X, ALU.max, negate=True))
                    nc.vector.tensor_tensor(logit[:, :, :], lg, ngate[:, :].unsqueeze(2).broadcast_to((128, TT, E)),
                                            ALU.add).then_inc(logits_ready, 1)
                if step == "route":
                    dve.wait_ge(probs_ready, b + 1)
                    own(nc.vector.tensor_reduce(psum_[:, :], prob[:, :, :], AX.X, ALU.add))
                    own(nc.vector.reciprocal(ngate[:, :], psum_[:, :]))
                    own(nc.vector.tensor_tensor(padded[:, :, 0:E], prob[:, :, :],
                                                     ngate[:, :].unsqueeze(2).broadcast_to((128, TT, E)), ALU.mult))
                    for t in range(TT):
                        ins = nc.vector.max(top[:, t, :], padded[:, t, :])
                    own(ins)
                    for t in range(TT):
                        ins = nc.vector.match_replace(rest[:, t, :], top[:, t, :], padded[:, t, :], 0.0)
                    own(ins)
                    own(nc.vector.tensor_reduce(psum_[:, :], top[:, :, PADS:8], AX.X, ALU.add))
                    own(nc.vector.tensor_scalar(psum_[:, :], psum_[:, :], TOP_EPS, None, ALU.add))
                    own(nc.vector.reciprocal(ngate[:, :], psum_[:, :]))
                    own(nc.vector.tensor_tensor(comb[:, :, 0:E], padded[:, :, 0:E], rest[:, :, 0:E],
                                                     ALU.subtract))
                    own(nc.vector.tensor_tensor(comb[:, :, 0:E], comb[:, :, 0:E],
                                                     ngate[:, :].unsqueeze(2).broadcast_to((128, TT, E)), ALU.mult))
                    own(nc.vector.tensor_copy(comb3[:, :, 0:EC], comb[:, :, :]))
                    own(nc.vector.tensor_tensor(comb_r[:, :, :], comb[:, :, :], comb3[:, :, 0:EC], ALU.subtract))
                    own(nc.vector.tensor_copy(comb3[:, :, EC:2 * EC], comb_r[:, :, :]))
                    nc.vector.tensor_tensor(comb3[:, :, 2 * EC:], comb_r[:, :, :], comb3[:, :, EC:2 * EC],
                                            ALU.subtract).then_inc(comb_ready, 1)

            def attention(b, p, front, tail):
                for step in ATTENTION:
                    if front:
                        front_work(step, b + 1, 1 - p)
                    if tail:
                        tail_work(step, b - 1, 1 - p)
                    if step[0] == "S":
                        g, j = int(step[1]), int(step[2])
                        dve.wait_ge(scores_done, G * J * b + J * g + j + 1)
                        pair = sc[j % 4][:, :].rearrange("p (c t) -> p c t", c=2)[:, :, 0:2 * QB * (j + 1)]
                        nc.vector.tensor_reduce(negmax[:, g, j, :], pair, AX.X, ALU.max,
                                                negate=True).then_inc(max_ready, 1)
                    if step[0] == "U" and int(step[2]) % 2 == 1:
                        copy_pt(dve, nc.vector.tensor_copy, b, int(step[1]), int(step[2]))
                    if step == "ln2a":
                        dve.wait_ge(pv_done, b + 1)
                        pv = acc[:, 0:TT * H * (DH + 1)].rearrange("p (n d) -> p n d", d=DH + 1)
                        own(nc.vector.reciprocal(rden[:, :], pv[:, :, DH]))
                        own(nc.vector.tensor_tensor(attn[:, :, :], pv[:, :, 0:DH],
                                                         rden[:, :].unsqueeze(2).broadcast_to((128, TT * H, DH)),
                                                         ALU.mult))
                        xb = x_s[:, bass.ds(b, 1), :]
                        nc.vector.scalar_tensor_tensor(out=xb, in0=attn[:, :, :].rearrange("p n d -> p (n d)").unsqueeze(1),
                                                       scalar=tanh_s[:, 0:1], in1=xb, op0=ALU.mult,
                                                       op1=ALU.add).then_inc(pv_read, 1)
                        dve.drain()
                        stats_of(b, stats2, mv2, var2, var2_ready)

            def experts(i):
                for e in range(EX):
                    dve.wait_ge(gelu_ready, EX * i + e + 1)
                    dve.wait_ge(up_half_done, EX * i + e + 1)
                    dst = act1 if e < E else act2
                    ins = nc.vector.scalar_tensor_tensor(out=dst[:, e % 2, :], in0=sc[2 * (e % 2)][:, :],
                                                         scalar=b1x_s[:, e:e + 1], in1=gelu_s[:, e % 2, :],
                                                         op0=ALU.add, op1=ALU.mult)
                    if e < E:
                        own(ins)
                        ins = nc.vector.tensor_tensor(act2[:, e % 2, :], act1[:, e % 2, :], tp[e % 2][:, :],
                                                      ALU.mult)
                    ins.then_inc(act_ready, 1)
                dve.wait_ge(yback_done, i + 1)
                xp = x_s[:, bass.ds(2 * i, 2), :]
                nc.vector.tensor_tensor(out_s[:, :].rearrange("p (b f) -> p b f", b=2),
                                        misc[:, :].rearrange("p (b f) -> p b f", b=2), xp,
                                        ALU.add).then_inc(out_ready, 1)

            dve.wait_ge(x_loaded, 16 * B)
            front_work("ln1a", 0, 0)
            front_work("ln1b", 0, 0)
            dve.wait_ge(attn_loaded, 16 * N_ATTN)
            nc.vector.tensor_copy(idb_s[:, :], id_s[:, :])
            nc.vector.tensor_copy(causal_s[:, :, :], causal_f[:, :, :]).then_inc(consts_ready, 1)
            front_work("q", 0, 0)
            front_work("v", 0, 0)
            dve.wait_ge(tanh_ready, 33)
            attention(0, 0, True, False)
            dve.wait_ge(moe_loaded, 16 * N_MOE)
            nc.vector.tensor_copy(oh_s[:, :, :], oh_f[:, :, :])
            nc.vector.tensor_tensor(w2_s[:, :, :], w2_s[:, :, :],
                                    mult_s[:, :].unsqueeze(2).broadcast_to((128, EX, D)),
                                    ALU.mult).then_inc(w2_scaled, 1)
            with dve.Fori(0, PAIRS - 1) as i:
                attention(2 * i + 1, 1, True, True)
                attention(2 * i + 2, 0, True, True)
                dve.wait_ge(out_free, i + 1)
                experts(i)
            attention(B - 1, 1, False, True)
            for step in ("ln2b", "gate", "route"):
                tail_work(step, B - 1, 1)
            dve.wait_ge(out_free, PAIRS)
            experts(PAIRS - 1)

        @block.tensor
        def _(pe):
            mm = nc.tensor.matmul

            def front_work(step, b, p, k):
                if step == "tr1":
                    pe.wait_ge(xn1_ready, b + 1)
                    for t in range(TT):
                        ins = nc.tensor.transpose(misc[:, t * 128:(t + 1) * 128], xn[:, t * 128:(t + 1) * 128],
                                                  id_s[:, :])
                    ins.then_inc(tr1_done, 1)
                if step == "q":
                    pe.wait_ge(xnT_ready, b + 1)
                    mm(misc[:, 0:S], wq_s[:, :], xnT[:, :], start=True, stop=True).then_inc(q_done, 1)
                if step == "k":
                    pe.wait_ge(q_ready, b + 1)
                    pe.wait_ge(ctx_loaded[p], 16 * (k + 1))
                    mm(misc[:, 0:S], wk_s[:, :], c_s[:, p, :], start=True, stop=True).then_inc(k_done, 1)
                if step == "v":
                    pe.wait_ge(k_ready, b + 1)
                    for t in range(TT):
                        ins = mm(misc[:, t * 128:(t + 1) * 128], c_s[:, p, t * 128:(t + 1) * 128], wv_s[:, :],
                                 start=True, stop=True)
                    ins.then_inc(v_done, 1)

            def tail_work(step, b, p):
                if step == "tr2":
                    pe.wait_ge(xn2_ready, b + 1)
                    for t in range(TT):
                        ins = nc.tensor.transpose(misc[:, t * 128:(t + 1) * 128], xn2[:, t * 128:(t + 1) * 128],
                                                  id_s[:, :])
                    ins.then_inc(tr2_done, 1)
                if step == "gate":
                    pe.wait_ge(x2T_ready, b + 1)
                    for t in range(TT):
                        ins = mm(misc[:, t * EC:t * EC + E], x2T[:, p * S + t * 128:p * S + (t + 1) * 128],
                                 gate_s[:, :], start=True, stop=True)
                    ins.then_inc(gate_done, 1)
                if step == "comb":
                    pe.wait_ge(comb_ready, b + 1)
                    for t in range(TT):
                        nc.tensor.transpose(misc[0:EC, S + t * 128:S + (t + 1) * 128], comb[:, t, :], id_s[:, :])
                    for t in range(TT):
                        ins = nc.tensor.transpose(misc[0:3 * EC, t * 64:(t + 1) * 64].bitcast(BF16),
                                                  comb3[:, t, :], idb_s[:, :])
                    ins.then_inc(combT_done, 1)

            def scores(b, p, g, j):
                bank = sc[j % 4]
                L = 2 * QB * (j + 1)
                rows = slice(64 * g, 64 * g + 64)
                for c in range(2):
                    q0 = 2 * QB * j + QB * c
                    o = bank[:, c * S:c * S + L]
                    mm(o, q_over_queries[:, p, 2 * j + c, HG * g:HG * (g + 1), :].rearrange("p h i -> p (h i)"), erw_s[:, S - 1 - q0:S - 1 - q0 + L],
                       start=True, stop=False)
                    mm(o, q_over_heads[rows, p, 2 * j + c, :, :].rearrange("p h i -> p (h i)"), kT[rows, p, 0:L], start=False, stop=False)
                    ins = mm(bank[:, c * S + L - 2 * QB:c * S + L], causal_s[:, c, :], idb_s[0:2 * QB, 0:2 * QB],
                             start=False, stop=True)
                ins.then_inc(scores_done, 1)

            def attention(b, p, k, front, tail, after_experts=None):
                first = True
                for step in ATTENTION:
                    if front and step == "tr1" and not tail:
                        pe.wait_ge(v_ready, b + 1)
                    if tail and step == "tr2":
                        pe.wait_ge(v_ready, b + 1)
                        pe.wait_ge(combT_ready, b)
                        if after_experts is not None:
                            pe.wait_ge(out_ready, after_experts + 1)
                    if tail and front and step == "tr1":
                        pe.wait_ge(logits_ready, b)
                    if tail and step == "comb" and front:
                        pe.wait_ge(v_ready, b + 2)
                    if tail:
                        tail_work(step, b - 1, 1 - p)
                    if front:
                        front_work(step, b + 1, 1 - p, k + p)
                    if step[0] == "S":
                        g, j = int(step[1]), int(step[2])
                        if g == 0 and j == 0:
                            pe.wait_ge(heads_ready, b + 1)
                            pe.wait_ge(k_ready, b + 1)
                            if after_experts is not None:
                                pe.wait_ge(act_ready, EX * after_experts + 1)
                        if j == 0:
                            pe.wait_ge(queries_ready, 4 * b + 2 * (g + 1))
                        if not (first and isinstance(b, int) and b == 0):
                            pe.wait_ge(exp_ready, G * J * b + J * g + j - 3)
                        if j == 3:
                            first = False
                        scores(b, p, g, j)
                    if step[0] == "U":
                        g, u = int(step[1]), int(step[2])
                        slot, kt, blk, last = UNITS[u]
                        pe.wait_ge(exp_ready, G * J * b + J * g + last + 1)
                        if not (isinstance(b, int) and b == 0 and g == 0 and u < 2):
                            pe.wait_ge(pt_ready[u % 2], 3 * (G * b + g) + u // 2)
                        for n in range(4):
                            ins = nc.tensor.transpose(tp[u % 2][:, n * 128:(n + 1) * 128],
                                                      p_s[:, g, blk + n, kt * 128:(kt + 1) * 128], id_s[:, :])
                        ins.then_inc(pt_done, 1)
                    if step[:2] == "PV":
                        g = int(step[2])
                        for s in pt_ready:
                            pe.wait_ge(s, 3 * (G * b + g + 1))
                        if g == 0:
                            pe.wait_ge(v_ready, b + 1)
                            if not (isinstance(b, int) and b == 0):
                                pe.wait_ge(pv_read, b)
                            if after_experts is not None:
                                pe.wait_ge(yT_ready, after_experts + 1)
                        for hh in range(HG):
                            h = HG * g + hh
                            for slot, qt, kt in SLOTS:
                                ins = mm(pv_v[:, qt, h, :], pt_s[:, g, slot, hh, :], v_s[:, p, kt, h, :],
                                         start=(kt == 0), stop=(kt == qt))
                        if g == G - 1:
                            ins.then_inc(pv_done, 1)

            def experts(i, b_last):
                def up(e):
                    gate_bank, up_bank = sc[2 * (e % 2) + 1], sc[2 * (e % 2)]
                    if e >= 2:
                        pe.wait_ge(act_ready, EX * i + e)
                    mm(gate_bank[:, :], w1_s[:, e, 128:256], x2T[:, :], start=True, stop=True)\
                        .then_inc(gate_half_done, 1)
                    if e < E:
                        mm(tp[e % 2][:, :], oh_s[:, e, :], comb3T[:, :], start=True, stop=True)
                    mm(up_bank[:, :], w1_s[:, e, 0:128], x2T[:, :], start=True, stop=True).then_inc(up_half_done, 1)

                def down(e):
                    pe.wait_ge(act_ready, EX * i + e + 2)
                    mm(acc[:, :], w2_s[:, e, :], act2[:, e % 2, :], start=(e == 0), stop=False)

                pe.wait_ge(combT_ready, 2 * i + 3)
                pe.wait_ge(exp_ready, G * J * (b_last + 1))
                pe.wait_ge(pv_read, b_last + 1)
                for e in range(EX):
                    up(e)
                    if e >= 1:
                        down(e - 1)
                down(EX - 1)
                mm(acc[:, :], b2_s[:, :], combT[:, :], start=False, stop=True).then_inc(y_done, 1)
                pe.wait_ge(yT_ready, i + 2)
                for n in range(2 * TT):
                    ins = nc.tensor.transpose(misc[:, n * 128:(n + 1) * 128], yT[:, n * 128:(n + 1) * 128], id_s[:, :])
                ins.then_inc(yback_done, 1)

            pe.wait_ge(attn_loaded, 16 * N_ATTN)
            pe.wait_ge(consts_ready, 1)
            for step in ("tr1", "q", "k", "v"):
                front_work(step, 0, 0, 0)
            attention(0, 0, 0, True, False)
            pe.wait_ge(moe_loaded, 16 * N_MOE)
            pe.wait_ge(w2_scaled, 1)
            with pe.Fori(0, PAIRS - 1) as i:
                attention(2 * i + 1, 1, i, True, True, after_experts=i)
                attention(2 * i + 2, 0, i + 1, True, True)
                pe.wait_ge(v_ready, 2 * i + 4)
                pe.wait_ge(combT_ready, 2 * i + 3)
                experts(i, 2 * i + 2)
            attention(B - 1, 1, PAIRS - 1, False, True, after_experts=PAIRS - 1)
            pe.wait_ge(combT_ready, B)
            for step in ("tr2", "gate", "comb"):
                if step == "comb":
                    pe.wait_ge(logits_ready, B)
                tail_work(step, B - 1, 1)
            experts(PAIRS - 1, B - 1)


_ARGS = ["x", "ctxT", "g_xattn", "g_ffn", "wqT", "bq", "wkT", "bk", "wvT", "bv", "erw", "gateT", "w1T", "b1x",
         "b1g", "mult", "w2T", "b2", "identity", "head_mask", "query_mask", "causal", "onehot"]


def kernel(**inputs):
    import numpy as np
    import concourse.bacc as bacc
    from concourse.bass_utils import run_bass_kernel_spmd as run

    a = {k: np.asarray(v) for k, v in inputs.items()}
    f32 = np.float32
    er = a["L0_xattn_Er"]
    erw = np.zeros((QB, DH, UW), f32)
    for i in range(QB):
        erw[i, :, i:i + S] = er.T[:, :UW - i]
    sf1, sf2 = a["L0_ffn_s_fc1_w"], a["L0_ffn_s_fc2_w"]
    sb1, sm = a["L0_ffn_s_fc1_b"], a["L0_ffn_s_geglu_mult"]
    s_w1 = np.stack([np.concatenate([sf1[n * 128:(n + 1) * 128], sf1[256 + n * 128:256 + (n + 1) * 128]])
                     for n in range(2)])
    s_b1 = np.stack([np.concatenate([sb1[n * 128:(n + 1) * 128], sb1[256 + n * 128:256 + (n + 1) * 128]])
                     for n in range(2)])
    w1 = np.concatenate([a["L0_ffn_fc1_w"], s_w1])
    b1 = np.concatenate([a["L0_ffn_fc1_b"], s_b1])
    w2 = np.concatenate([a["L0_ffn_fc2_w"], sf2[:, 0:128][None], sf2[:, 128:256][None]])
    mult = np.concatenate([a["L0_ffn_geglu_mult"], sm.reshape(2, 128)])
    head_mask = np.zeros((128, HG), f32)
    query_mask = np.zeros((128, QB), f32)
    causal = np.zeros((2 * QB, 2, 128), f32)
    onehot = np.zeros((3 * EC, E, 128), f32)
    for r in range(128):
        head_mask[r, r // DH % HG] = 1
        query_mask[r, r // DH] = 1
        for c in range(2):
            causal[r % QB + QB * c + 1:, c, r] = MASKED
    for e in range(E):
        onehot[e::EC, e, :] = 1
    arrays = {
        "x": a["x"], "ctxT": a["ctx_1024"].reshape(B * S, D).T, "g_xattn": a["g_xattn"], "g_ffn": a["g_ffn"],
        "wqT": a["L0_xattn_Wq"].T, "bq": a["L0_xattn_bq"].reshape(D, 1), "wkT": a["L0_xattn_Wk"].T,
        "bk": a["L0_xattn_bk"].reshape(D, 1), "wvT": a["L0_xattn_Wv"].T, "bv": a["L0_xattn_bv"],
        "erw": erw.reshape(QB * DH, UW), "gateT": a["L0_ffn_gate_w"].T, "w1T": w1.transpose(2, 0, 1),
        "b1x": b1[:, 0:128].T, "b1g": b1[:, 128:256].T, "mult": mult.T, "w2T": w2.transpose(2, 0, 1),
        "b2": np.concatenate([a["L0_ffn_fc2_b"], a["L0_ffn_s_fc2_b"][None]]), "identity": np.eye(128, dtype=f32),
        "head_mask": head_mask, "query_mask": query_mask, "causal": causal, "onehot": onehot,
    }
    arrays = {f"in_{k}": np.ascontiguousarray(v) for k, v in arrays.items()}
    nc = bacc.Bacc("TRN2", target_bir_lowering=False, num_devices=1)
    args = [nc.dram_tensor(f"in_{k}", arrays[f"in_{k}"].shape, F32, kind="ExternalInput").ap() for k in _ARGS]
    out = nc.dram_tensor("out", (B, S, D), F32, kind="ExternalOutput").ap()
    flamingo_block(nc, *args, out)
    return run(nc, [arrays], core_ids=[0]).results[0]["out"]
```

```python
from contextlib import ExitStack

import concourse.bass as bass
from concourse import mybir

F32 = mybir.dt.float32
BF16 = mybir.dt.bfloat16
F16 = mybir.dt.float16
ALU = mybir.AluOpType
ACT = mybir.ActivationFunctionType
AX = mybir.AxisListType

B, S, D = 8, 256, 128
H, DH = 16, 8
QB = 16
HG = 128 // QB
G = H // HG
NB = S // QB
J = S // (2 * QB)
TT = S // 128
E, TOPK = 15, 3
EX = E + 2
EC = E + 1
PAIRS = B // 2
PT_ = 2 * S
UW = S - 1 + 2 * QB
PADS = 8 - TOPK
PAD_VALUE = 2.0
EPS = 1e-5
TOP_EPS = 1e-20
MASKED = -1e30

ATTENTION = [
    "S00", "ln1a", "W0", "S01", "W1", "S02", "W2", "W3", "S03", "ln1b", "W4", "S04", "W5", "tr1", "S05",
    "VW", "NW", "S06", "q", "S07", "k", "ln2b", "S10", "U0", "tr2", "S11", "U1", "v", "S12", "gate", "U2", "U3",
    "S13", "heads", "U4", "route", "S14", "U5", "S15", "V0", "N0", "mask", "S16", "comb", "S17",
]
UNITS = [(0, 0, 0, 1), (0, 0, 4, 3), (1, 0, 8, 5), (2, 1, 8, 5), (1, 0, 12, 7), (2, 1, 12, 7)]
SLOTS = [(0, 0, 0), (1, 1, 0), (2, 1, 1)]


def flamingo_block(nc, x, ctxT, g_xattn, g_ffn, wqT, bq, wkT, bk, wvT, bv, erw, gateT,
                   w1T, b1x, b1g, mult, w2T, b2, identity, identity16, head_mask, query_mask, causal, onehot, out):
    with ExitStack() as ctx:
        def sb(name, shape, dt=F32):
            return ctx.enter_context(nc.sbuf_tensor(name, shape, dt))

        def sem(name):
            return ctx.enter_context(nc.semaphore(name))

        wq_s, wk_s, wv_s = sb("wq_s", [D, G, 128]), sb("wk_s", [D, G, 128]), sb("wv_s", [D, D])
        bq_s, bk_s = sb("bq_s", [128, G]), sb("bk_s", [128, G])
        bv_s = sb("bv_s", [128, D])
        erw_s, erw_h, erw_l = sb("erw_s", [128, UW]), sb("erw_h", [128, UW], F16), sb("erw_l", [128, UW], F16)
        gate_s, gate_h, gate_l = sb("gate_s", [D, E]), sb("gate_h", [D, E], F16), sb("gate_l", [D, E], F16)
        w1_h, w1_l, w2_s = sb("w1_h", [D, EX, 256], F16), sb("w1_l", [D, EX, 256], F16), sb("w2_s", [128, EX, D])
        b1x_s, b1g_s, mult_s = sb("b1x_s", [128, EX]), sb("b1g_s", [128, EX]), sb("mult_s", [128, EX])
        b2_s = sb("b2_s", [EC, D])
        id_s, id16_s = sb("id_s", [128, 128]), sb("id16_s", [128, 128], F16)
        hm_s, qm_s = sb("hm_s", [128, 128], F16), sb("qm_s", [128, QB], F16)
        causal_f, causal_s = sb("causal_f", [2 * QB, 2, 128]), sb("causal_s", [2 * QB, 2, 128], BF16)
        oh_s = sb("oh_s", [3 * EC, E, 128], F16)
        g_s, tanh_s = sb("g_s", [128, 2]), sb("tanh_s", [128, 2])
        half_s = sb("half_s", [128, TT])
        x_s = sb("x_s", [128, B, S])
        stats, mv, var, rstd = (sb("stats", [128, TT, 6]), sb("mv", [128, TT, 2]), sb("var", [128, TT]),
                                sb("rstd", [128, TT]))
        stats2, mv2, var2, rstd2 = (sb("stats2", [128, TT, 6]), sb("mv2", [128, TT, 2]), sb("var2", [128, TT]),
                                    sb("rstd2", [128, TT]))
        xn, xn2 = sb("xn", [128, S]), sb("xn2", [128, S])
        xnT = sb("xnT", [D, S])
        c_s = sb("c_s", [D, 2, S])
        q_s = sb("q_s", [128, 2, G, S], F16)
        k_h, k_l = sb("k_h", [128, 2, G, S], F16), sb("k_l", [64, 2, G, S], F16)
        q_over_heads = sb("q_over_heads", [128, 2, G, NB, 128], F16)
        q_spread_s = sb("q_spread_s", [128, 4 * HG, S], F16)
        q_over_queries = sb("q_over_queries", [128, 2, G, 2, NB, 128], F16)
        v_f, v_s = sb("v_f", [128, S]), sb("v_s", [128, 2, TT, H, 2 * DH + 1], F16)
        negmax = sb("negmax", [128, G, J, 2])
        p_f = sb("p_f", [128, 4, 2, S])
        p_s = sb("p_s", [128, G, 2 * J, 2, S], F16)
        pt_s = sb("pt_s", [128, 3, 2, HG, 128], F16)
        pv_s, rden, attn = sb("pv_s", [128, TT * HG, DH]), sb("rden", [128, TT * HG]), sb("attn", [128, TT, H, DH])
        x2_h, x2_l = sb("x2_h", [D, PT_], F16), sb("x2_l", [D, PT_], F16)
        ngate, logit, prob = sb("ngate", [128, TT]), sb("logit", [128, TT, E]), sb("prob", [128, TT, E])
        psum_, top, rest = sb("psum_", [128, TT]), sb("top", [128, TT, 8]), sb("rest", [128, TT, E + PADS])
        padded = sb("padded", [128, TT, E + PADS])
        comb, comb_r, comb3 = (sb("comb", [128, TT, EC]), sb("comb_r", [128, TT, EC]),
                               sb("comb3", [128, TT, 3 * EC], F16))
        combT, comb3T = sb("combT", [EC, PT_]), sb("comb3T", [3 * EC, PT_], F16)
        work = sb("work", [128, EX * 256])
        w1_stage = work[:, :].rearrange("p (e f) -> p e f", e=EX)
        gelu_s, act1, act2 = (work[:, n * 2 * PT_:(n + 1) * 2 * PT_].rearrange("p (r t) -> p r t", r=2)
                              for n in range(3))
        yT, out_s = work[:, 6 * PT_:7 * PT_], work[:, 7 * PT_:8 * PT_]
        q_dram = nc.dram_tensor("q_scratch", (2, G * 128, S), F16, kind="Internal").ap()

        sc = [ctx.enter_context(nc.psum_tensor(f"sc{i}", [128, 512], F32)) for i in range(4)]
        tp = [ctx.enter_context(nc.psum_tensor(f"tp{i}", [128, 512], F32)) for i in range(2)]
        acc = ctx.enter_context(nc.psum_tensor("acc", [128, 512], F32))
        misc = ctx.enter_context(nc.psum_tensor("misc", [128, 512], F32))
        pv_v = acc[:, 0:TT * HG * (2 * DH + 1)].rearrange("p (t h d) -> p t h d", t=TT, h=HG)

        attn_loaded, x0_loaded, x_loaded, moe_loaded = (sem("attn_loaded"), sem("x0_loaded"), sem("x_loaded"),
                                                    sem("moe_loaded"))
        ctx_loaded = [sem(f"ctx_loaded{p}") for p in range(2)]
        q_stored = [sem(f"q_stored{p}") for p in range(2)]
        q_spread = [sem(f"q_spread{p}") for p in range(2)]
        out_stored, out_free = sem("out_stored"), sem("out_free")
        consts_ready, gains_loaded, gains_ready, w1_split, w2_scaled, half_ready = (
            sem("consts_ready"), sem("gains_loaded"), sem("gains_ready"), sem("w1_split"), sem("w2_scaled"),
            sem("half_ready"))
        var1_ready, rstd1_ready, xn1_ready = sem("var1_ready"), sem("rstd1_ready"), sem("xn1_ready")
        tr1_done, xnT_ready = sem("tr1_done"), sem("xnT_ready")
        q_done, q_high, q_ready, k_done, k_high, k_ready, v_done, v_ready = (
            sem("q_done"), sem("q_high"), sem("q_ready"), sem("k_done"), sem("k_high"), sem("k_ready"),
            sem("v_done"), sem("v_ready"))
        heads_ready, queries_ready = sem("heads_ready"), sem("queries_ready")
        scores_done, max_ready, exp_ready, high_ready, low_ready = (
            sem("scores_done"), sem("max_ready"), sem("exp_ready"), sem("high_ready"), sem("low_ready"))
        pt_done = sem("pt_done")
        pt_ready = [sem("pt_ready_act"), sem("pt_ready_dve")]
        pv_done, pv_read = sem("pv_done"), sem("pv_read")
        var2_ready, rstd2_ready, xn2_ready = sem("var2_ready"), sem("rstd2_ready"), sem("xn2_ready")
        tr2_done, x2_high, x2_ready, gate_done, logits_ready, probs_ready = (
            sem("tr2_done"), sem("x2_high"), sem("x2_ready"), sem("gate_done"), sem("logits_ready"),
            sem("probs_ready"))
        comb_ready, combT_done, combT_ready = sem("comb_ready"), sem("combT_done"), sem("combT_ready")
        gate_half_done, up_half_done, gelu_ready, act_ready, y_done, yT_ready, yback_done, out_ready = (
            sem("gate_half_done"), sem("up_half_done"), sem("gelu_ready"), sem("act_ready"), sem("y_done"),
            sem("yT_ready"), sem("yback_done"), sem("out_ready"))
        block = ctx.enter_context(nc.Block())

        N_ATTN, N_MOE = 12, 8
        x_view = x.rearrange("b (t p) d -> p b t d", p=128)
        out_view = out.rearrange("b (t p) d -> p b t d", p=128)

        def unit(step):
            return step[0] == "W", int(step[0] == "W"), int(step[1])

        def copy_pt(eng, copy, b, g, u):
            eng.wait_ge(pt_done, len(UNITS) * (G * b + g) + u + 1)
            slot, _, blk, _ = UNITS[u]
            q0 = blk % 8 * QB
            dst = pt_s[:, slot, :, :, q0:q0 + 4 * QB].rearrange("p c h (k i) -> p (c h) k i", k=4)
            src = tp[u % 2][:, :].bitcast(F16).rearrange("p (k m i) -> p m k i", k=4, i=QB)
            copy(dst, src).then_inc(pt_ready[u % 2], 1)

        @block.sync
        def _(sp):
            def load_ctx(at, p):
                sp.dma_start(c_s[:, p, :], ctxT[:, bass.ds(at, S)]).then_inc(ctx_loaded[p], 16)

            def load_x(first, end, loaded):
                sp.dma_start(x_s[:, first:end, :].rearrange("p b (t d) -> p b t d", t=TT),
                             x_view[:, first:end]).then_inc(loaded, 16)

            def spread_q(b, p, k):
                sp.wait_ge(q_ready, b + 1)
                sp.wait_ge(queries_ready, b + 1)
                sp.dma_start(q_dram[p].rearrange("(g p) s -> p g s", g=G), q_s[:, p, :, :]).then_inc(q_stored[p], 16)
                sp.wait_ge(q_stored[p], 16 * (k + 1))
                src = q_dram[p].rearrange("(n d) s -> d n s", d=DH)
                for i in range(QB):
                    sp.dma_start(q_spread_s[i * DH:(i + 1) * DH, :, :], src).then_inc(q_spread[p], 16)

            sp.sem_inc(out_free, 1)
            load_x(0, 1, x0_loaded)
            sp.dma_start(id_s[:, :], identity).then_inc(attn_loaded, 16)
            sp.dma_start(wq_s[:, :, :], wqT).then_inc(attn_loaded, 16)
            sp.dma_start(bq_s[:, :], bq).then_inc(attn_loaded, 16)
            sp.dma_start(wk_s[:, :, :], wkT).then_inc(attn_loaded, 16)
            load_ctx(0, 0)
            for dst, src in ((bk_s, bk), (wv_s, wvT), (hm_s, head_mask), (qm_s, query_mask), (erw_s, erw),
                             (id16_s, identity16)):
                sp.dma_start(dst[:, :], src).then_inc(attn_loaded, 16)
            sp.dma_start(causal_f[:, :, :], causal).then_inc(attn_loaded, 16)
            sp.dma_start(bv_s[:, :], bv.partition_broadcast(128)).then_inc(attn_loaded, 16)
            load_ctx(S, 1)
            spread_q(0, 0, 0)
            load_x(1, B, x_loaded)
            for dst, src in ((gate_s, gateT), (b1x_s, b1x), (b1g_s, b1g), (mult_s, mult), (b2_s, b2)):
                sp.dma_start(dst[:, :], src).then_inc(moe_loaded, 16)
            for dst, src in ((w1_stage, w1T), (w2_s, w2T), (oh_s, onehot)):
                sp.dma_start(dst[:, :, :], src).then_inc(moe_loaded, 16)
            spread_q(1, 1, 0)
            with sp.Fori(0, PAIRS - 1) as i:
                even, odd, pair = sp.snap((2 * i + 2) * S), sp.snap((2 * i + 3) * S), sp.snap(2 * i)
                sp.wait_ge(v_ready, 2 * i + 1)
                load_ctx(even, 0)
                spread_q(2 * i + 2, 0, i + 1)
                sp.wait_ge(v_ready, 2 * i + 2)
                load_ctx(odd, 1)
                spread_q(2 * i + 3, 1, i + 1)
                sp.wait_ge(out_ready, i + 2)
                sp.dma_start(out_view[:, bass.ds(pair, 2)],
                             out_s.rearrange("p (b t d) -> p b t d", b=2, t=TT)).then_inc(out_stored, 16)
                sp.wait_ge(out_stored, 16 * (i + 1))
                sp.sem_inc(out_free, 1)
            sp.wait_ge(out_ready, PAIRS + 1)
            sp.dma_start(out_view[:, B - 2:B],
                         out_s.rearrange("p (b t d) -> p b t d", b=2, t=TT)).then_inc(out_stored, 16)
            sp.wait_ge(out_stored, 16 * PAIRS)

        @block.gpsimd
        def _(pool):
            nc.gpsimd.memset(half_s[:, :], -0.5).then_inc(half_ready, 1)
            pool.wait_ge(half_ready, 1)

            def rsqrt(v, r, ready_in, ready_out, b):
                pool.wait_ge(ready_in, b + 1)
                nc.gpsimd.tensor_tensor(r[:, :], v[:, :], half_s[:, :], ALU.pow).then_inc(ready_out, 1)

            def attention(b, front, tail):
                for step in ATTENTION:
                    if front and step == "ln1a":
                        rsqrt(var, rstd, var1_ready, rstd1_ready, b + 1)
                    if tail and step == "NW":
                        rsqrt(var2, rstd2, var2_ready, rstd2_ready, b - 1)
                    if step[0] == "S":
                        g, j = int(step[1]), int(step[2])
                        L = 2 * QB * (j + 1)
                        pool.wait_ge(high_ready, G * J * b + J * g + j + 1)
                        nc.gpsimd.tensor_tensor(p_s[:, g, 2 * j:2 * j + 2, 1, 0:L], p_f[:, j % 4, :, 0:L],
                                                p_s[:, g, 2 * j:2 * j + 2, 0, 0:L], ALU.subtract)\
                            .then_inc(low_ready, 1)

            rsqrt(var, rstd, var1_ready, rstd1_ready, 0)
            attention(0, True, False)
            with pool.Fori(0, PAIRS - 1) as i:
                attention(2 * i + 1, True, True)
                attention(2 * i + 2, True, True)
            attention(B - 1, False, True)
            rsqrt(var2, rstd2, var2_ready, rstd2_ready, B - 1)

        @block.scalar
        def _(act):
            act.dma_start(g_s[:, 0:1], g_xattn.partition_broadcast(128)).then_inc(gains_loaded, 16)
            act.dma_start(g_s[:, 1:2], g_ffn.partition_broadcast(128)).then_inc(gains_loaded, 16)
            act.wait_ge(gains_loaded, 32)
            nc.scalar.activation(tanh_s[:, :], g_s[:, :], ACT.Tanh).then_inc(gains_ready, 1)
            act.sem_inc(combT_ready, 1)
            act.sem_inc(yT_ready, 1)
            act.wait_ge(attn_loaded, 16 * N_ATTN)
            act.wait_ge(consts_ready, 1)

            def front_work(step, b, p):
                if step == "tr1":
                    act.wait_ge(tr1_done, b + 1)
                    nc.scalar.copy(xnT[:, :], misc[:, 0:S]).then_inc(xnT_ready, 1)
                if step in "qk":
                    done, dst, bias, high = ((q_done, q_s, bq_s, q_high) if step == "q" else
                                             (k_done, k_h, bk_s, k_high))
                    act.wait_ge(done, b + 1)
                    for g in range(G):
                        ins = nc.scalar.activation(dst[:, p, g, :], misc[:, g * S:(g + 1) * S], ACT.Identity,
                                                   bias=bias[:, g:g + 1])
                    ins.then_inc(high, 1)

            def tail_work(step, b, p):
                if step == "tr2":
                    act.wait_ge(tr2_done, b + 1)
                    nc.scalar.copy(x2_h[:, p * S:(p + 1) * S], misc[:, 0:S]).then_inc(x2_high, 1)
                if step == "route":
                    act.wait_ge(logits_ready, b + 1)
                    nc.scalar.activation(prob[:, :, :], logit[:, :, :], ACT.Exp).then_inc(probs_ready, 1)
                if step == "comb":
                    act.wait_ge(combT_done, b + 1)
                    nc.scalar.copy(comb3T[:, p * S:(p + 1) * S], misc[0:3 * EC, 0:S // 2].bitcast(F16))
                    nc.scalar.copy(combT[:, p * S:(p + 1) * S], misc[0:EC, S:2 * S]).then_inc(combT_ready, 1)

            def attention(b, p, front, tail):
                for step in ATTENTION:
                    if front:
                        front_work(step, b + 1, 1 - p)
                    if tail:
                        tail_work(step, b - 1, 1 - p)
                    if step[0] == "S":
                        g, j = int(step[1]), int(step[2])
                        n = G * J * b + J * g + j
                        act.wait_ge(max_ready, n + 1)
                        if not (isinstance(b, int) and n < 4):
                            act.wait_ge(low_ready, n - 3)
                        L = 2 * QB * (j + 1)
                        for c in range(2):
                            ins = nc.scalar.activation(p_f[:, j % 4, c, 0:L], sc[j % 4][:, c * S:c * S + L],
                                                       ACT.Exp, bias=negmax[:, g, j, c:c + 1])
                        ins.then_inc(exp_ready, 1)
                        act.wait_ge(exp_ready, n + 1)
                        nc.scalar.copy(p_s[:, g, 2 * j:2 * j + 2, 0, 0:L], p_f[:, j % 4, :, 0:L])\
                            .then_inc(high_ready, 1)
                    if step[0] in "UW" and int(step[1]) % 2 == 0:
                        before, g, u = unit(step)
                        if tail or not before:
                            copy_pt(act, nc.scalar.copy, b - before, g, u)

            def experts(i):
                for e in range(EX):
                    act.wait_ge(gate_half_done, EX * i + e + 1)
                    nc.scalar.activation(gelu_s[:, e % 2, :], sc[2 * (e % 2) + 1][:, :], ACT.Gelu,
                                         bias=b1g_s[:, e:e + 1]).then_inc(gelu_ready, 1)
                act.wait_ge(y_done, i + 1)
                nc.scalar.activation(yT, acc[:, :], ACT.Identity, scale=tanh_s[:, 1:2]).then_inc(yT_ready, 1)

            for step in ("tr1", "q", "k"):
                front_work(step, 0, 0)
            attention(0, 0, True, False)
            act.wait_ge(moe_loaded, 16 * N_MOE)
            act.wait_ge(w1_split, 1)
            with act.Fori(0, PAIRS - 1) as i:
                attention(2 * i + 1, 1, True, True)
                attention(2 * i + 2, 0, True, True)
                experts(i)
            attention(B - 1, 1, False, True)
            for u in (0, 2, 4):
                copy_pt(act, nc.scalar.copy, B - 1, 1, u)
            for step in ("tr2", "route", "comb"):
                tail_work(step, B - 1, 1)
            experts(PAIRS - 1)

        @block.vector
        def _(dve):
            def own(ins):
                dve.drain()

            dve.sem_inc(act_ready, 1)
            dve.sem_inc(out_ready, 1)
            dve.sem_inc(queries_ready, 1)

            def stats_of(b, st, m, v, ready):
                for t in range(TT):
                    ins = nc.vector.bn_stats(st[:, t, :], x_s[:, bass.ds(b, 1), t * 128:(t + 1) * 128])
                own(ins)
                for t in range(TT):
                    ins = nc.vector.bn_aggr(m[:, t, :], st[:, t, :])
                own(ins)
                nc.vector.tensor_scalar(v[:, :], m[:, :, 1], EPS, None, ALU.add).then_inc(ready, 1)

            def normalise(b, m, r, dst, ready):
                for t in range(TT):
                    ins = nc.vector.tensor_scalar(dst[:, t * 128:(t + 1) * 128],
                                                  x_s[:, bass.ds(b, 1), t * 128:(t + 1) * 128],
                                                  m[:, t, 0:1], r[:, t:t + 1], ALU.subtract, ALU.mult)
                ins.then_inc(ready, 1)

            def low_part(dst, src, bias, high, rows, p, ready):
                for g in range(G):
                    ins = nc.vector.scalar_tensor_tensor(out=dst[rows, p, g, :], in0=src[rows, g * S:(g + 1) * S],
                                                         scalar=bias[rows, g:g + 1], in1=high[rows, p, g, :],
                                                         op0=ALU.add, op1=ALU.subtract)
                ins.then_inc(ready, 1)

            def front_work(step, b, p, k):
                if step == "ln1a":
                    dve.wait_ge(x0_loaded if isinstance(b, int) and b == 0 else x_loaded, 16)
                    stats_of(b, stats, mv, var, var1_ready)
                if step == "ln1b":
                    dve.wait_ge(rstd1_ready, b + 1)
                    normalise(b, mv, rstd, xn, xn1_ready)
                if step == "q":
                    dve.wait_ge(q_high, b + 1)
                    low_part(q_s, misc, bq_s, q_s, slice(64, 128), p, q_ready)
                if step == "k":
                    dve.wait_ge(k_high, b + 1)
                    low_part(k_l, misc, bk_s, k_h, slice(0, 64), p, k_ready)
                if step == "heads":
                    for g in range(G):
                        ins = nc.vector.tensor_tensor(
                            q_over_heads[:, p, g, :, :].rearrange("p k (h i) -> p k h i", h=HG),
                            q_s[:, p, g, :].rearrange("p (k i) -> p k i", i=QB).unsqueeze(2)
                            .broadcast_to((128, NB, HG, QB)),
                            hm_s[:, :].rearrange("p (h i) -> p h i", h=HG).unsqueeze(1)
                            .broadcast_to((128, NB, HG, QB)), ALU.mult)
                    ins.then_inc(heads_ready, 1)
                if step == "mask":
                    dve.wait_ge(q_spread[p], 16 * QB * (k + 1))
                    for n in range(2 * G):
                        ins = nc.vector.tensor_tensor(
                            q_over_queries[:, p, n // 2, n % 2, :, :].rearrange("p k (h i) -> p k h i", h=HG),
                            q_spread_s[:, HG * n:HG * (n + 1), :].rearrange("p h (k i) -> p k h i", i=QB),
                            qm_s[:, :].unsqueeze(1).unsqueeze(1).broadcast_to((128, NB, HG, QB)), ALU.mult)
                    ins.then_inc(queries_ready, 1)
                if step == "v":
                    dve.wait_ge(v_done, b + 1)
                    own(nc.vector.tensor_tensor(v_f[:, :].rearrange("p (t f) -> p t f", t=TT),
                                                misc[:, 0:S].rearrange("p (t f) -> p t f", t=TT),
                                                bv_s[:, :].unsqueeze(1).broadcast_to((128, TT, D)), ALU.add))
                    vf = v_f[:, :].rearrange("p (n d) -> p n d", d=DH)
                    vs = v_s[:, p, :, :, :].rearrange("p t h d -> p (t h) d")
                    own(nc.vector.tensor_copy(vs[:, :, 0:DH], vf))
                    nc.vector.tensor_tensor(vs[:, :, DH:2 * DH], vf, vs[:, :, 0:DH], ALU.subtract)\
                        .then_inc(v_ready, 1)

            def tail_work(step, b, p):
                if step == "ln2b":
                    dve.wait_ge(rstd2_ready, b + 1)
                    normalise(b, mv2, rstd2, xn2, xn2_ready)
                if step == "tr2":
                    dve.wait_ge(x2_high, b + 1)
                    cols = slice(p * S, (p + 1) * S)
                    nc.vector.tensor_tensor(x2_l[:, cols], misc[:, 0:S], x2_h[:, cols],
                                            ALU.subtract).then_inc(x2_ready, 1)
                if step == "gate":
                    dve.wait_ge(gate_done, b + 1)
                    lg = misc[:, 0:TT * EC].rearrange("p (t e) -> p t e", t=TT)[:, :, 0:E]
                    own(nc.vector.tensor_reduce(ngate[:, :], lg, AX.X, ALU.max, negate=True))
                    nc.vector.tensor_tensor(logit[:, :, :], lg, ngate[:, :].unsqueeze(2).broadcast_to((128, TT, E)),
                                            ALU.add).then_inc(logits_ready, 1)
                if step == "route":
                    dve.wait_ge(probs_ready, b + 1)
                    own(nc.vector.tensor_reduce(psum_[:, :], prob[:, :, :], AX.X, ALU.add))
                    own(nc.vector.reciprocal(ngate[:, :], psum_[:, :]))
                    own(nc.vector.tensor_tensor(padded[:, :, 0:E], prob[:, :, :],
                                                ngate[:, :].unsqueeze(2).broadcast_to((128, TT, E)), ALU.mult))
                    for t in range(TT):
                        ins = nc.vector.max(top[:, t, :], padded[:, t, :])
                    own(ins)
                    for t in range(TT):
                        ins = nc.vector.match_replace(rest[:, t, :], top[:, t, :], padded[:, t, :], 0.0)
                    own(ins)
                    nc.vector.tensor_tensor(comb[:, :, 0:E], padded[:, :, 0:E], rest[:, :, 0:E], ALU.subtract)
                    own(nc.vector.tensor_reduce(psum_[:, :], top[:, :, PADS:8], AX.X, ALU.add))
                    own(nc.vector.tensor_scalar(psum_[:, :], psum_[:, :], TOP_EPS, None, ALU.add))
                    own(nc.vector.reciprocal(ngate[:, :], psum_[:, :]))
                    own(nc.vector.tensor_tensor(comb[:, :, 0:E], comb[:, :, 0:E],
                                                ngate[:, :].unsqueeze(2).broadcast_to((128, TT, E)), ALU.mult))
                    own(nc.vector.tensor_copy(comb3[:, :, 0:EC], comb[:, :, :]))
                    own(nc.vector.tensor_tensor(comb_r[:, :, :], comb[:, :, :], comb3[:, :, 0:EC], ALU.subtract))
                    own(nc.vector.tensor_copy(comb3[:, :, EC:2 * EC], comb_r[:, :, :]))
                    nc.vector.tensor_tensor(comb3[:, :, 2 * EC:], comb_r[:, :, :], comb3[:, :, EC:2 * EC],
                                            ALU.subtract).then_inc(comb_ready, 1)

            def normalise_heads(b, g):
                dve.wait_ge(pv_done, G * b + g + 1)
                pv = acc[:, 0:TT * HG * (2 * DH + 1)].rearrange("p (n d) -> p n d", d=2 * DH + 1)
                nc.vector.reciprocal(rden[:, :], pv[:, :, 2 * DH])
                own(nc.vector.tensor_reduce(pv_s[:, :, :],
                                            pv[:, :, 0:2 * DH].rearrange("p n (c d) -> p n d c", c=2), AX.X,
                                            ALU.add))
                nc.vector.tensor_tensor(attn[:, :, HG * g:HG * (g + 1), :],
                                        pv_s[:, :, :].rearrange("p (t h) d -> p t h d", t=TT),
                                        rden[:, :].rearrange("p (t h) -> p t h", t=TT).unsqueeze(3)
                                        .broadcast_to((128, TT, HG, DH)), ALU.mult).then_inc(pv_read, 1)
                if g == G - 1:
                    dve.drain()
                    xb = x_s[:, bass.ds(b, 1), :]
                    own(nc.vector.scalar_tensor_tensor(
                        out=xb, in0=attn[:, :, :, :].rearrange("p t h d -> p (t h d)").unsqueeze(1),
                        scalar=tanh_s[:, 0:1], in1=xb, op0=ALU.mult, op1=ALU.add))
                    stats_of(b, stats2, mv2, var2, var2_ready)

            def attention(b, p, k, front, tail):
                for step in ATTENTION:
                    if front:
                        front_work(step, b + 1, 1 - p, k + p)
                    if tail:
                        tail_work(step, b - 1, 1 - p)
                    if step[0] == "S":
                        g, j = int(step[1]), int(step[2])
                        dve.wait_ge(scores_done, G * J * b + J * g + j + 1)
                        pair = sc[j % 4][:, :].rearrange("p (c t) -> p c t", c=2)[:, :, 0:2 * QB * (j + 1)]
                        nc.vector.tensor_reduce(negmax[:, g, j, :], pair, AX.X, ALU.max,
                                                negate=True).then_inc(max_ready, 1)
                    if step[0] in "UW" and int(step[1]) % 2 == 1:
                        before, g, u = unit(step)
                        if tail or not before:
                            copy_pt(dve, nc.vector.tensor_copy, b - before, g, u)
                    if step == "N0":
                        normalise_heads(b, 0)
                    if step == "NW" and tail:
                        normalise_heads(b - 1, 1)

            def experts(i):
                for e in range(EX):
                    dve.wait_ge(gelu_ready, EX * i + e + 1)
                    dve.wait_ge(up_half_done, EX * i + e + 1)
                    dst = act1 if e < E else act2
                    ins = nc.vector.scalar_tensor_tensor(out=dst[:, e % 2, :], in0=sc[2 * (e % 2)][:, :],
                                                         scalar=b1x_s[:, e:e + 1], in1=gelu_s[:, e % 2, :],
                                                         op0=ALU.add, op1=ALU.mult)
                    if e < E:
                        own(ins)
                        ins = nc.vector.tensor_tensor(act2[:, e % 2, :], act1[:, e % 2, :], tp[e % 2][:, :],
                                                      ALU.mult)
                    ins.then_inc(act_ready, 1)
                dve.wait_ge(yback_done, i + 1)
                xp = x_s[:, bass.ds(2 * i, 2), :]
                nc.vector.tensor_tensor(out_s.rearrange("p (b f) -> p b f", b=2),
                                        misc[:, :].rearrange("p (b f) -> p b f", b=2), xp,
                                        ALU.add).then_inc(out_ready, 1)

            front_work("ln1a", 0, 0, 0)
            nc.vector.memset(v_s[:, :, :, :, 2 * DH:], 1.0)
            nc.vector.memset(padded[:, :, E:], PAD_VALUE)
            nc.vector.memset(comb[:, :, E:], 1.0)
            nc.vector.memset(p_s[:, :, :, :, :].bitcast(F32), 0.0)
            front_work("ln1b", 0, 0, 0)
            dve.wait_ge(attn_loaded, 16 * N_ATTN)
            nc.vector.tensor_scalar(wq_s[:, :, :], wq_s[:, :, :], DH ** -0.5, None, ALU.mult)
            nc.vector.tensor_scalar(bq_s[:, :], bq_s[:, :], DH ** -0.5, None, ALU.mult)
            nc.vector.tensor_copy(causal_s[:, :, :], causal_f[:, :, :])
            own(nc.vector.tensor_copy(erw_h[:, :], erw_s[:, :]))
            nc.vector.tensor_tensor(erw_l[:, :], erw_s[:, :], erw_h[:, :], ALU.subtract).then_inc(consts_ready, 1)
            for step in ("q", "k", "v", "heads", "mask"):
                front_work(step, 0, 0, 0)
            dve.wait_ge(gains_ready, 1)
            attention(0, 0, 0, True, False)
            dve.wait_ge(moe_loaded, 16 * N_MOE)
            nc.vector.tensor_copy(gate_h[:, :], gate_s[:, :])
            own(nc.vector.tensor_copy(w1_h[:, :, :], w1_stage))
            nc.vector.tensor_tensor(gate_l[:, :], gate_s[:, :], gate_h[:, :], ALU.subtract)
            nc.vector.tensor_tensor(w1_l[:, :, :], w1_stage, w1_h[:, :, :], ALU.subtract).then_inc(w1_split, 1)
            nc.vector.tensor_tensor(w2_s[:, :, :], w2_s[:, :, :],
                                    mult_s[:, :].unsqueeze(2).broadcast_to((128, EX, D)),
                                    ALU.mult).then_inc(w2_scaled, 1)
            with dve.Fori(0, PAIRS - 1) as i:
                attention(2 * i + 1, 1, i, True, True)
                attention(2 * i + 2, 0, i + 1, True, True)
                dve.wait_ge(out_free, i + 1)
                experts(i)
            attention(B - 1, 1, PAIRS - 1, False, True)
            for u in (1, 3, 5):
                copy_pt(dve, nc.vector.tensor_copy, B - 1, 1, u)
            normalise_heads(B - 1, 1)
            for step in ("ln2b", "tr2", "gate", "route"):
                tail_work(step, B - 1, 1)
            dve.wait_ge(out_free, PAIRS)
            experts(PAIRS - 1)

        @block.tensor
        def _(pe):
            mm = nc.tensor.matmul

            def three(out_, stat_h, stat_l, mov_h, mov_l, start=True, stop=True):
                mm(out_, stat_h, mov_h, start=start, stop=False)
                mm(out_, stat_h, mov_l, start=False, stop=False)
                return mm(out_, stat_l, mov_h, start=False, stop=stop)

            def front_work(step, b, p, k):
                if step == "tr1":
                    pe.wait_ge(xn1_ready, b + 1)
                    for t in range(TT):
                        ins = nc.tensor.transpose(misc[:, t * 128:(t + 1) * 128], xn[:, t * 128:(t + 1) * 128],
                                                  id_s[:, :])
                    ins.then_inc(tr1_done, 1)
                if step == "q":
                    pe.wait_ge(xnT_ready, b + 1)
                    for g in range(G):
                        ins = mm(misc[:, g * S:(g + 1) * S], wq_s[:, g, :], xnT[:, :], start=True, stop=True)
                    ins.then_inc(q_done, 1)
                if step == "k":
                    pe.wait_ge(q_ready, b + 1)
                    pe.wait_ge(ctx_loaded[p], 16 * (k + 1))
                    for g in range(G):
                        ins = mm(misc[:, g * S:(g + 1) * S], wk_s[:, g, :], c_s[:, p, :], start=True, stop=True)
                    ins.then_inc(k_done, 1)
                if step == "v":
                    pe.wait_ge(k_ready, b + 1)
                    for t in range(TT):
                        ins = mm(misc[:, t * 128:(t + 1) * 128], c_s[:, p, t * 128:(t + 1) * 128], wv_s[:, :],
                                 start=True, stop=True)
                    ins.then_inc(v_done, 1)

            def tail_work(step, b, p):
                if step == "tr2":
                    pe.wait_ge(xn2_ready, b + 1)
                    for t in range(TT):
                        ins = nc.tensor.transpose(misc[:, t * 128:(t + 1) * 128], xn2[:, t * 128:(t + 1) * 128],
                                                  id_s[:, :])
                    ins.then_inc(tr2_done, 1)
                if step == "gate":
                    pe.wait_ge(x2_ready, b + 1)
                    for t in range(TT):
                        cols = slice(p * S + t * 128, p * S + (t + 1) * 128)
                        ins = three(misc[:, t * EC:t * EC + E], x2_h[:, cols], x2_l[:, cols], gate_h[:, :],
                                    gate_l[:, :])
                    ins.then_inc(gate_done, 1)
                if step == "comb":
                    pe.wait_ge(comb_ready, b + 1)
                    for t in range(TT):
                        nc.tensor.transpose(misc[0:EC, S + t * 128:S + (t + 1) * 128], comb[:, t, :], id_s[:, :])
                    for t in range(TT):
                        ins = nc.tensor.transpose(misc[0:3 * EC, t * 64:(t + 1) * 64].bitcast(F16),
                                                  comb3[:, t, :], id16_s[:, :])
                    ins.then_inc(combT_done, 1)

            def scores(p, g, j):
                bank = sc[j % 4]
                L = 2 * QB * (j + 1)
                for c in range(2):
                    n = 2 * j + c
                    u0 = S - 1 - QB * n
                    o = bank[:, c * S:c * S + L]
                    mm(o, q_over_queries[:, p, g, 0, n, :], erw_h[:, u0:u0 + L], start=True, stop=False)
                    mm(o, q_over_queries[:, p, g, 0, n, :], erw_l[:, u0:u0 + L], start=False, stop=False)
                    mm(o, q_over_queries[:, p, g, 1, n, :], erw_h[:, u0:u0 + L], start=False, stop=False)
                    mm(o, q_over_heads[:, p, g, n, :], k_h[:, p, g, 0:L], start=False, stop=False)
                    mm(o, q_over_heads[0:64, p, g, n, :], k_l[:, p, g, 0:L], start=False, stop=False)
                    ins = mm(bank[:, c * S + L - 2 * QB:c * S + L], causal_s[:, c, :], id16_s[0:2 * QB, 0:2 * QB],
                             start=False, stop=True)
                ins.then_inc(scores_done, 1)

            def transposes(b, g, u):
                slot, kt, blk, last = UNITS[u]
                pe.wait_ge(low_ready, G * J * b + J * g + last + 1)
                if not (isinstance(b, int) and b == 0 and g == 0 and u < 2):
                    pe.wait_ge(pt_ready[u % 2], 3 * (G * b + g) + u // 2)
                for n in range(4):
                    for c in range(2):
                        at = 64 * (2 * n + c)
                        ins = nc.tensor.transpose(tp[u % 2][:, at:at + 64].bitcast(F16),
                                                  p_s[:, g, blk + n, c, kt * 128:(kt + 1) * 128], id16_s[:, :])
                ins.then_inc(pt_done, 1)

            def values(b, p, g, after_experts=None):
                for s in pt_ready:
                    pe.wait_ge(s, 3 * (G * b + g + 1))
                if not (isinstance(b, int) and b == 0 and g == 0):
                    pe.wait_ge(pv_read, G * b + g)
                if after_experts is not None:
                    pe.wait_ge(yT_ready, after_experts + 1)
                for hh in range(HG):
                    for slot, qt, kt in SLOTS:
                        for c in range(2):
                            ins = mm(pv_v[:, qt, hh, :], pt_s[:, slot, c, hh, :], v_s[:, p, kt, HG * g + hh, :],
                                     start=(kt == 0 and c == 0), stop=(kt == qt and c == 1))
                ins.then_inc(pv_done, 1)

            def attention(b, p, k, front, tail, after_experts=None):
                for step in ATTENTION:
                    if step == ("tr1" if front else "tr2"):
                        pe.wait_ge(v_ready, b + 1)
                        if tail:
                            pe.wait_ge(combT_ready, b)
                        if after_experts is not None:
                            pe.wait_ge(out_ready, after_experts + 1)
                    if tail and front and step == "tr2":
                        pe.wait_ge(k_ready, b + 2)
                    if tail and front and step == "v":
                        pe.wait_ge(x2_ready, b)
                    if tail and front and step == "gate":
                        pe.wait_ge(v_ready, b + 2)
                    if tail and step == "comb":
                        pe.wait_ge(logits_ready, b)
                    if tail:
                        tail_work(step, b - 1, 1 - p)
                    if front:
                        front_work(step, b + 1, 1 - p, k + p)
                    if step[0] == "S":
                        g, j = int(step[1]), int(step[2])
                        if g == 0 and j == 0:
                            pe.wait_ge(heads_ready, b + 1)
                            pe.wait_ge(queries_ready, b + 2)
                            pe.wait_ge(k_ready, b + 1)
                            if after_experts is not None:
                                pe.wait_ge(act_ready, EX * after_experts + 1)
                        n = G * J * b + J * g + j
                        if not (isinstance(b, int) and n < 4):
                            pe.wait_ge(exp_ready, n - 3)
                        scores(p, g, j)
                    if step[0] in "UW":
                        before, g, u = unit(step)
                        if tail or not before:
                            transposes(b - before, g, u)
                    if step == "V0":
                        values(b, p, 0)
                    if step == "VW" and tail:
                        values(b - 1, 1 - p, 1, after_experts)

            def experts(i, b_last, groups):
                def up(e):
                    gate_bank, up_bank = sc[2 * (e % 2) + 1], sc[2 * (e % 2)]
                    if e >= 2:
                        pe.wait_ge(act_ready, EX * i + e)
                    three(gate_bank[:, :], w1_h[:, e, 128:256], w1_l[:, e, 128:256], x2_h[:, :], x2_l[:, :])\
                        .then_inc(gate_half_done, 1)
                    if e < E:
                        mm(tp[e % 2][:, :], oh_s[:, e, :], comb3T[:, :], start=True, stop=True)
                    three(up_bank[:, :], w1_h[:, e, 0:128], w1_l[:, e, 0:128], x2_h[:, :], x2_l[:, :])\
                        .then_inc(up_half_done, 1)

                def down(e):
                    pe.wait_ge(act_ready, EX * i + e + 2)
                    mm(acc[:, :], w2_s[:, e, :], act2[:, e % 2, :], start=(e == 0), stop=False)

                pe.wait_ge(combT_ready, 2 * i + 3)
                pe.wait_ge(exp_ready, G * J * (b_last + 1))
                for s in pt_ready:
                    pe.wait_ge(s, 3 * groups)
                pe.wait_ge(pv_read, groups)
                for e in range(EX):
                    up(e)
                    if e >= 1:
                        down(e - 1)
                down(EX - 1)
                mm(acc[:, :], b2_s[:, :], combT[:, :], start=False, stop=True).then_inc(y_done, 1)
                pe.wait_ge(yT_ready, i + 2)
                for n in range(2 * TT):
                    ins = nc.tensor.transpose(misc[:, n * 128:(n + 1) * 128], yT[:, n * 128:(n + 1) * 128], id_s[:, :])
                ins.then_inc(yback_done, 1)

            pe.wait_ge(attn_loaded, 16 * N_ATTN)
            pe.wait_ge(consts_ready, 1)
            for step in ("tr1", "q", "k", "v"):
                front_work(step, 0, 0, 0)
            attention(0, 0, 0, True, False)
            pe.wait_ge(moe_loaded, 16 * N_MOE)
            pe.wait_ge(w1_split, 1)
            pe.wait_ge(w2_scaled, 1)
            with pe.Fori(0, PAIRS - 1) as i:
                attention(2 * i + 1, 1, i, True, True, after_experts=i)
                attention(2 * i + 2, 0, i + 1, True, True)
                experts(i, 2 * i + 2, G * (2 * i + 2) + 1)
            attention(B - 1, 1, PAIRS - 1, False, True, after_experts=PAIRS - 1)
            for u in range(len(UNITS)):
                transposes(B - 1, 1, u)
            values(B - 1, 1, 1)
            pe.wait_ge(combT_ready, B)
            tail_work("tr2", B - 1, 1)
            tail_work("gate", B - 1, 1)
            pe.wait_ge(logits_ready, B)
            tail_work("comb", B - 1, 1)
            experts(PAIRS - 1, B - 1, G * B)


_ARGS = ["x", "ctxT", "g_xattn", "g_ffn", "wqT", "bq", "wkT", "bk", "wvT", "bv", "erw", "gateT", "w1T", "b1x",
         "b1g", "mult", "w2T", "b2", "identity", "identity16", "head_mask", "query_mask", "causal", "onehot"]


def kernel(**inputs):
    import numpy as np
    import concourse.bacc as bacc
    from concourse.bass_utils import run_bass_kernel_spmd as run

    a = {k: np.asarray(v) for k, v in inputs.items()}
    f32 = np.float32
    er = a["L0_xattn_Er"]
    erw = np.zeros((QB, DH, UW), f32)
    for i in range(QB):
        erw[i, :, i:i + S] = er.T[:, :UW - i]
    sf1, sf2 = a["L0_ffn_s_fc1_w"], a["L0_ffn_s_fc2_w"]
    sb1, sm = a["L0_ffn_s_fc1_b"], a["L0_ffn_s_geglu_mult"]
    s_w1 = np.stack([np.concatenate([sf1[n * 128:(n + 1) * 128], sf1[256 + n * 128:256 + (n + 1) * 128]])
                     for n in range(2)])
    s_b1 = np.stack([np.concatenate([sb1[n * 128:(n + 1) * 128], sb1[256 + n * 128:256 + (n + 1) * 128]])
                     for n in range(2)])
    w1 = np.concatenate([a["L0_ffn_fc1_w"], s_w1])
    b1 = np.concatenate([a["L0_ffn_fc1_b"], s_b1])
    w2 = np.concatenate([a["L0_ffn_fc2_w"], sf2[:, 0:128][None], sf2[:, 128:256][None]])
    mult = np.concatenate([a["L0_ffn_geglu_mult"], sm.reshape(2, 128)])
    head_mask = np.zeros((128, HG, QB), np.float16)
    query_mask = np.zeros((128, QB), np.float16)
    causal = np.zeros((2 * QB, 2, 128), f32)
    onehot = np.zeros((3 * EC, E, 128), np.float16)
    for r in range(128):
        head_mask[r, r // DH % HG] = 1
        query_mask[r, r // DH] = 1
        for c in range(2):
            causal[r % QB + QB * c + 1:, c, r] = MASKED
    twice = lambda w: np.stack([np.concatenate([w[64 * g:64 * g + 64]] * 2) for g in range(G)])
    for e in range(E):
        onehot[e::EC, e, :] = 1
    arrays = {
        "x": a["x"], "ctxT": a["ctx_1024"].reshape(B * S, D).T, "g_xattn": a["g_xattn"], "g_ffn": a["g_ffn"],
        "wqT": twice(a["L0_xattn_Wq"]).transpose(2, 0, 1), "bq": twice(a["L0_xattn_bq"]).T,
        "wkT": twice(a["L0_xattn_Wk"]).transpose(2, 0, 1),
        "bk": twice(a["L0_xattn_bk"]).T, "wvT": a["L0_xattn_Wv"].T, "bv": a["L0_xattn_bv"],
        "erw": erw.reshape(QB * DH, UW), "gateT": a["L0_ffn_gate_w"].T, "w1T": w1.transpose(2, 0, 1),
        "b1x": b1[:, 0:128].T, "b1g": b1[:, 128:256].T, "mult": mult.T, "w2T": w2.transpose(2, 0, 1),
        "b2": np.concatenate([a["L0_ffn_fc2_b"], a["L0_ffn_s_fc2_b"][None]]), "identity": np.eye(128, dtype=f32), "identity16": np.eye(128, dtype=np.float16),
        "head_mask": head_mask.reshape(128, 128), "query_mask": query_mask, "causal": causal, "onehot": onehot,
    }
    arrays = {f"in_{k}": np.ascontiguousarray(v) for k, v in arrays.items()}
    nc = bacc.Bacc("TRN2", target_bir_lowering=False, num_devices=1)
    args = [nc.dram_tensor(f"in_{k}", arrays[f"in_{k}"].shape, mybir.dt.from_np(arrays[f"in_{k}"].dtype), kind="ExternalInput").ap() for k in _ARGS]
    out = nc.dram_tensor("out", (B, S, D), F32, kind="ExternalOutput").ap()
    flamingo_block(nc, *args, out)
    return run(nc, [arrays], core_ids=[0]).results[0]["out"]
```

```python
from contextlib import ExitStack

import concourse.bass as bass
from concourse import mybir

F32 = mybir.dt.float32
BF16 = mybir.dt.bfloat16
F16 = mybir.dt.float16
ALU = mybir.AluOpType
ACT = mybir.ActivationFunctionType
AX = mybir.AxisListType

B, S, D = 8, 256, 128
H, DH = 16, 8
QB = 16
HG = 128 // QB
G = H // HG
NB = S // QB
J = S // (2 * QB)
TT = S // 128
E, TOPK = 15, 3
EX = E + 2
EC = E + 1
PAIRS = B // 2
LEAD = 3
LAG = 3
PT_ = 2 * S
UW = S - 1 + 2 * QB
PADS = 8 - TOPK
PAD_VALUE = 2.0
EPS = 1e-5
TOP_EPS = 1e-20
MASKED = -1e30

TENSOR_ORDER = [
    "W0", "W1", "S00", "S01", "S02", "W2", "W3", "S03", "W4", "S04", "tr1", "W5", "q", "k", "S05", "VW",
    "S06", "U0", "U1", "v", "S07", "S10", "U2", "U3", "S11", "tr2", "gate", "S12", "S13", "S14", "U4", "U5",
    "comb", "S15", "V0", "S16", "S17",
]
SCALAR_ORDER = [
    "S00", "S01", "W0", "W1", "S02", "W2", "W3", "S03", "W4", "S04", "tr1", "W5", "q", "S05", "k", "S06",
    "U0", "U1", "S07", "S10", "U2", "U3", "S11", "tr2", "S12", "route", "S13", "S14", "U4", "U5", "S15",
    "S16", "S17", "comb",
]
VECTOR_ORDER = [
    "ln1a", "S00", "W0", "W1", "S01", "S02", "W2", "W3", "S03", "S04", "W4", "W5", "S05", "ql", "S06", "S07",
    "kl", "NW", "U0", "heads0", "U1", "S10", "v", "S11", "U2", "S12", "x2l", "S13", "U3", "gate", "S14",
    "route", "U4", "U5", "S15", "S16", "S17", "N0",
]
GPSIMD_ORDER = [
    "ln1a", "own0", "ln1b", "own1", "own2", "own3", "own4", "own5", "own6", "own7", "heads1", "NW", "ln2b",
    "mask0", "mask1", "mask2", "mask3", "mask4", "mask5", "mask6", "mask7",
]
UNITS = [(0, 0, 0, 1), (0, 0, 4, 3), (1, 0, 8, 5), (2, 1, 8, 5), (1, 0, 12, 7), (2, 1, 12, 7)]
SLOTS = [(0, 0, 0), (1, 1, 0), (2, 1, 1)]


def flamingo_block(nc, x, ctxT, g_xattn, g_ffn, wqT, bq, wkT, bk, wvT, bv, erw, gateT,
                   w1T, b1x, b1g, mult, w2T, b2, identity, identity16, head_mask, query_mask, causal, onehot, out):
    with ExitStack() as ctx:
        def sb(name, shape, dt=F32):
            return ctx.enter_context(nc.sbuf_tensor(name, shape, dt))

        def sem(name):
            return ctx.enter_context(nc.semaphore(name))

        wq_s, wk_s, wv_s = sb("wq_s", [D, G, 128]), sb("wk_s", [D, G, 128]), sb("wv_s", [D, D])
        bq_s, bk_s = sb("bq_s", [128, G]), sb("bk_s", [128, G])
        bv_s = sb("bv_s", [128, D])
        erw_h, erw_l = sb("erw_h", [128, UW], F16), sb("erw_l", [128, UW], F16)
        gate_s, gate_h, gate_l = sb("gate_s", [D, E]), sb("gate_h", [D, E], F16), sb("gate_l", [D, E], F16)
        w1_h, w1_l, w2_s = sb("w1_h", [D, EX, 256], F16), sb("w1_l", [D, EX, 256], F16), sb("w2_s", [128, EX, D])
        w2_h, w2_l = sb("w2_h", [128, EX, D], F16), sb("w2_l", [128, EX, D], F16)
        b1x_s, b1g_s, mult_s = sb("b1x_s", [128, EX]), sb("b1g_s", [128, EX]), sb("mult_s", [128, EX])
        b2_s = sb("b2_s", [EC, D])
        id_s, id16_s = sb("id_s", [128, 128]), sb("id16_s", [128, 128], F16)
        hm_s, qm_s = sb("hm_s", [128, 128], F16), sb("qm_s", [128, QB], F16)
        causal_s = sb("causal_s", [2 * QB, 2, 128], BF16)
        oh_s = sb("oh_s", [3 * EC, E, 128], F16)
        g_s, tanh_s = sb("g_s", [128, 2]), sb("tanh_s", [128, 2])
        half_s = sb("half_s", [128, TT])
        x_s = sb("x_s", [128, B, S])
        stats, mv, var, rstd = (sb("stats", [128, TT, 6]), sb("mv", [128, TT, 2]), sb("var", [128, TT]),
                                sb("rstd", [128, TT]))
        stats2, mv2, var2, rstd2 = (sb("stats2", [128, TT, 6]), sb("mv2", [128, TT, 2]), sb("var2", [128, TT]),
                                    sb("rstd2", [128, TT]))
        xn = sb("xn", [128, S])
        xnT = sb("xnT", [D, S])
        c_s = sb("c_s", [D, 2, S])
        q_s = sb("q_s", [128, 2, G, S], F16)
        k_h, k_l = sb("k_h", [128, 2, G, S], F16), sb("k_l", [64, 2, G, S], F16)
        q_over_heads = sb("q_over_heads", [128, 2, G, NB, 128], F16)
        q_spread_s = sb("q_spread_s", [128, 4 * HG, S], F16)
        q_over_queries = sb("q_over_queries", [128, 2, G, 2, NB, 128], F16)
        v_f, v_s = sb("v_f", [128, S]), sb("v_s", [128, 2, TT, H, 2 * DH + 1], F16)
        negmax = sb("negmax", [128, G, J, 2])
        p_s = sb("p_s", [128, G, 2 * J, S])
        stage = sb("stage", [128, UW + 2 * 128])
        erw_s = stage[:, 0:UW]
        causal_f = stage[0:2 * QB, UW:].rearrange("p (c r) -> p c r", c=2)
        pt_s = sb("pt_s", [128, 3, 2, HG, 128], F16)
        pv_s, rden, attn = sb("pv_s", [128, TT * HG, DH]), sb("rden", [128, TT * HG]), sb("attn", [128, TT, H, DH])
        x2_h, x2_l = sb("x2_h", [D, PT_], F16), sb("x2_l", [D, PT_], F16)
        ngate, logit, prob = sb("ngate", [128, TT]), sb("logit", [128, TT, E]), sb("prob", [128, TT, E])
        psum_, top, rest = sb("psum_", [128, TT]), sb("top", [128, TT, 8]), sb("rest", [128, TT, E + PADS])
        padded = sb("padded", [128, TT, E + PADS])
        comb, comb_r, comb3 = (sb("comb", [128, TT, EC]), sb("comb_r", [128, TT, EC]),
                               sb("comb3", [128, TT, 3 * EC], F16))
        combT, comb3T = sb("combT", [EC, PT_]), sb("comb3T", [3 * EC, PT_], F16)
        work = sb("work", [128, EX * 256])
        w1_stage = work[:, :].rearrange("p (e f) -> p e f", e=EX)
        gelu_s, act2 = (work[:, n * PT_:(n + 2) * PT_].rearrange("p (r t) -> p r t", r=2) for n in (0, 2))
        out_s, yT = work[:, 4 * PT_:5 * PT_], gelu_s[:, 1, :]
        act_parts = work[:, 5 * PT_:8 * PT_].bitcast(F16).rearrange("p (r c t) -> p r c t", r=LAG, c=2)
        q_dram = nc.dram_tensor("q_scratch", (2, DH, 4 * HG, S), F16, kind="Internal").ap()

        sc = [ctx.enter_context(nc.psum_tensor(f"sc{i}", [128, 512], F32)) for i in range(4)]
        tp = [ctx.enter_context(nc.psum_tensor(f"tp{i}", [128, 512], F32)) for i in range(2)]
        acc = ctx.enter_context(nc.psum_tensor("acc", [128, 512], F32))
        misc = ctx.enter_context(nc.psum_tensor("misc", [128, 512], F32))
        pv_v = acc[:, 0:TT * HG * (2 * DH + 1)].rearrange("p (t h d) -> p t h d", t=TT, h=HG)

        id_loaded, wq_loaded = sem("id_loaded"), sem("wq_loaded")
        attn_loaded, x0_loaded, x_loaded, moe_loaded = (sem("attn_loaded"), sem("x0_loaded"), sem("x_loaded"),
                                                    sem("moe_loaded"))
        ctx_loaded = [sem(f"ctx_loaded{p}") for p in range(2)]
        q_stored = [sem(f"q_stored{p}") for p in range(2)]
        q_spread = [[sem(f"q_spread{p}_{g}") for g in range(G)] for p in range(2)]
        out_stored, out_free = sem("out_stored"), sem("out_free")
        probs_cleared, wq_scaled, gate_split = sem("probs_cleared"), sem("wq_scaled"), sem("gate_split")
        w_high = sem("w_high")
        consts_ready, gains_loaded, gains_ready, experts_split, half_ready = (
            sem("consts_ready"), sem("gains_loaded"), sem("gains_ready"), sem("experts_split"), sem("half_ready"))
        centred1, centred2 = sem("centred1"), sem("centred2")
        var1_ready, rstd1_ready, xn1_ready = sem("var1_ready"), sem("rstd1_ready"), sem("xn1_ready")
        tr1_done, xnT_ready = sem("tr1_done"), sem("xnT_ready")
        q_done, q_high, q_ready, k_done, k_high, k_ready, v_done, v_ready = (
            sem("q_done"), sem("q_high"), sem("q_ready"), sem("k_done"), sem("k_high"), sem("k_ready"),
            sem("v_done"), sem("v_ready"))
        heads_ready = [sem(f"heads_ready{g}") for g in range(G)]
        queries_ready = [sem(f"queries_ready{g}") for g in range(G)]
        scores_done, max_ready, exp_ready = sem("scores_done"), sem("max_ready"), sem("exp_ready")
        pt_done = sem("pt_done")
        pt_high, pt_ready = sem("pt_high"), sem("pt_ready")
        pv_done, pv_read = sem("pv_done"), sem("pv_read")
        var2_ready, rstd2_ready, xn2_ready = sem("var2_ready"), sem("rstd2_ready"), sem("xn2_ready")
        tr2_done, x2_high, x2_ready, gate_done, logits_ready, probs_ready = (
            sem("tr2_done"), sem("x2_high"), sem("x2_ready"), sem("gate_done"), sem("logits_ready"),
            sem("probs_ready"))
        comb_ready, combT_done, combT_ready = sem("comb_ready"), sem("combT_done"), sem("combT_ready")
        gate_half_done, up_half_done, weights_done, gelu_ready = (
            sem("gate_half_done"), sem("up_half_done"), sem("weights_done"), sem("gelu_ready"))
        act_ready, act_high, act_split, down_done = (
            sem("act_ready"), sem("act_high"), sem("act_split"), sem("down_done"))
        y_done, yT_ready, yback_done, out_ready = (
            sem("y_done"), sem("yT_ready"), sem("yback_done"), sem("out_ready"))
        block = ctx.enter_context(nc.Block())

        N_ATTN, N_MOE = 9, 8
        x_view = x.rearrange("b (t p) d -> p b t d", p=128)
        out_view = out.rearrange("b (t p) d -> p b t d", p=128)

        def unit(step):
            return step[0] == "W", int(step[0] == "W"), int(step[1])

        def head_block(eng, p, g):
            eng.tensor_tensor(
                q_over_heads[:, p, g, :, :].rearrange("p k (h i) -> p k h i", h=HG),
                q_s[:, p, g, :].rearrange("p (k i) -> p k i", i=QB).unsqueeze(2).broadcast_to((128, NB, HG, QB)),
                hm_s[:, :].rearrange("p (h i) -> p h i", h=HG).unsqueeze(1).broadcast_to((128, NB, HG, QB)),
                ALU.mult).then_inc(heads_ready[g], 1)

        def pt_parts(g, u):
            slot, _, blk, _ = UNITS[u]
            q0 = blk % 8 * QB
            src = tp[u % 2][:, :].rearrange("p (k h i) -> p h k i", k=4, i=QB)
            high, low = (pt_s[:, slot, c, :, q0:q0 + 4 * QB].rearrange("p h (k i) -> p h k i", k=4)
                         for c in range(2))
            return src, high, low

        @block.sync
        def _(sp):
            def load_ctx(at, p):
                sp.dma_start(c_s[:, p, :], ctxT[:, bass.ds(at, S)]).then_inc(ctx_loaded[p], 16)

            def load_x(first, end, loaded):
                sp.dma_start(x_s[:, first:end, :].rearrange("p b (t d) -> p b t d", t=TT),
                             x_view[:, first:end]).then_inc(loaded, 16)

            def spread_q(b, p, k):
                sp.wait_ge(q_ready, b + 1)
                for masked in queries_ready:
                    sp.wait_ge(masked, b + 1)
                for g in range(G):
                    sp.dma_start(q_dram[p][:, 2 * HG * g:2 * HG * (g + 1), :].transpose([1, 0, 2]), q_s[:, p, g, :])\
                        .then_inc(q_stored[p], 16)
                sp.wait_ge(q_stored[p], 16 * G * (k + 1))
                for g in range(G):
                    rows = slice(2 * HG * g, 2 * HG * (g + 1))
                    sp.dma_start(q_spread_s[:, rows, :].rearrange("p n s -> p (n s)"),
                                 q_dram[p][:, rows, :].rearrange("d n s -> d (n s)").unsqueeze(0)
                                 .broadcast_to((QB, DH, 2 * HG * S))).then_inc(q_spread[p][g], 16)

            sp.sem_inc(out_free, 1)
            load_x(0, 1, x0_loaded)
            sp.dma_start(id_s[:, :], identity).then_inc(id_loaded, 16)
            sp.dma_start(wq_s[:, :, :], wqT).then_inc(wq_loaded, 16)
            sp.dma_start(bq_s[:, :], bq).then_inc(wq_loaded, 16)
            sp.dma_start(wk_s[:, :, :], wkT).then_inc(attn_loaded, 16)
            load_ctx(0, 0)
            for dst, src in ((bk_s, bk), (wv_s, wvT), (hm_s, head_mask), (qm_s, query_mask), (erw_s, erw),
                             (id16_s, identity16)):
                sp.dma_start(dst[:, :], src).then_inc(attn_loaded, 16)
            sp.dma_start(causal_f[:, :, :], causal).then_inc(attn_loaded, 16)
            sp.dma_start(bv_s[:, :], bv.partition_broadcast(128)).then_inc(attn_loaded, 16)
            load_ctx(S, 1)
            spread_q(0, 0, 0)
            load_x(1, B, x_loaded)
            for dst, src in ((gate_s, gateT), (b1x_s, b1x), (b1g_s, b1g), (mult_s, mult), (b2_s, b2)):
                sp.dma_start(dst[:, :], src).then_inc(moe_loaded, 16)
            for dst, src in ((w1_stage, w1T), (w2_s, w2T), (oh_s, onehot)):
                sp.dma_start(dst[:, :, :], src).then_inc(moe_loaded, 16)
            spread_q(1, 1, 0)
            with sp.Fori(0, PAIRS - 1) as i:
                even, odd, pair = sp.snap((2 * i + 2) * S), sp.snap((2 * i + 3) * S), sp.snap(2 * i)
                sp.wait_ge(v_ready, 2 * i + 1)
                load_ctx(even, 0)
                spread_q(2 * i + 2, 0, i + 1)
                sp.wait_ge(v_ready, 2 * i + 2)
                load_ctx(odd, 1)
                spread_q(2 * i + 3, 1, i + 1)
                sp.wait_ge(out_ready, i + 2)
                sp.dma_start(out_view[:, bass.ds(pair, 2)],
                             out_s.rearrange("p (b t d) -> p b t d", b=2, t=TT)).then_inc(out_stored, 16)
                sp.wait_ge(out_stored, 16 * (i + 1))
                sp.sem_inc(out_free, 1)
            sp.wait_ge(out_ready, PAIRS + 1)
            sp.dma_start(out_view[:, B - 2:B],
                         out_s.rearrange("p (b t d) -> p b t d", b=2, t=TT)).then_inc(out_stored, 16)
            sp.wait_ge(out_stored, 16 * PAIRS)

        @block.gpsimd
        def _(pool):
            pool.sem_inc(queries_ready[1], 1)
            nc.gpsimd.memset(half_s[:, :], -0.5).then_inc(half_ready, 1)
            pool.wait_ge(half_ready, 1)

            def rsqrt(v, r, ready_in, ready_out, b):
                pool.wait_ge(ready_in, b + 1)
                nc.gpsimd.tensor_tensor(r[:, :], v[:, :], half_s[:, :], ALU.pow).then_inc(ready_out, 1)

            def normalise(b, m, r, ready_in, centred, ready_out):
                xc = xn[:, :].rearrange("p (t f) -> p t f", t=TT)
                nc.gpsimd.tensor_tensor(xc, x_s[:, bass.ds(b, 1), :].rearrange("p o (t f) -> p (o t) f", t=TT),
                                        m[:, :, 0:1].broadcast_to((128, TT, 128)), ALU.subtract)\
                    .then_inc(centred, 1)
                pool.wait_ge(centred, b + 1)
                pool.wait_ge(ready_in, b + 1)
                nc.gpsimd.tensor_tensor(xc, xc, r[:, :].unsqueeze(2).broadcast_to((128, TT, 128)), ALU.mult)\
                    .then_inc(ready_out, 1)

            def mask(p, k, n):
                g, part, h0 = n // 8, n // 4 % 2, n % 4 * 2
                if n % 8 == 0:
                    pool.wait_ge(q_spread[p][g], 16 * (k + 1))
                at = HG * (2 * g + part) + h0
                ins = nc.gpsimd.tensor_tensor(
                    q_over_queries[:, p, g, part, :, h0 * QB:(h0 + 2) * QB].rearrange("p k (h i) -> p k h i", h=2),
                    q_spread_s[:, at:at + 2, :].rearrange("p h (k i) -> p k h i", i=QB),
                    qm_s[:, :].unsqueeze(1).unsqueeze(1).broadcast_to((128, NB, 2, QB)), ALU.mult)
                if n % 8 == 7:
                    ins.then_inc(queries_ready[g], 1)

            def attention(b, p, k, front, tail):
                for step in GPSIMD_ORDER:
                    if front and step == "ln1a":
                        rsqrt(var, rstd, var1_ready, rstd1_ready, b + 1)
                    if front and step == "ln1b":
                        normalise(b + 1, mv, rstd, rstd1_ready, centred1, xn1_ready)
                    if tail and step == "NW":
                        rsqrt(var2, rstd2, var2_ready, rstd2_ready, b - 1)
                    if tail and step == "ln2b":
                        normalise(b - 1, mv2, rstd2, rstd2_ready, centred2, xn2_ready)
                    if front and step == "heads1":
                        pool.wait_ge(q_ready, b + 2)
                        head_block(nc.gpsimd, 1 - p, 1)
                    if front and step[:4] == "mask":
                        mask(1 - p, k + p, int(step[4:]))
                    if step[:3] == "own":
                        mask(p, k, 8 + int(step[3:]))

            def experts(i):
                for e in range(EX):
                    pool.wait_ge(act_high, EX * i + e + 1)
                    nc.gpsimd.tensor_tensor(act_parts[:, e % LAG, 1, :], act2[:, e % 2, :],
                                            act_parts[:, e % LAG, 0, :], ALU.subtract).then_inc(act_split, 1)

            rsqrt(var, rstd, var1_ready, rstd1_ready, 0)
            normalise(0, mv, rstd, rstd1_ready, centred1, xn1_ready)
            nc.gpsimd.memset(p_s[:, :, :, :], 0.0).then_inc(probs_cleared, 1)
            pool.wait_ge(probs_cleared, 1)
            pool.wait_ge(attn_loaded, 16 * N_ATTN)
            attention(0, 0, 0, True, False)
            with pool.Fori(0, PAIRS - 1) as i:
                attention(2 * i + 1, 1, i, True, True)
                attention(2 * i + 2, 0, i + 1, True, True)
                experts(i)
            attention(B - 1, 1, PAIRS - 1, False, True)
            rsqrt(var2, rstd2, var2_ready, rstd2_ready, B - 1)
            normalise(B - 1, mv2, rstd2, rstd2_ready, centred2, xn2_ready)
            experts(PAIRS - 1)

        @block.scalar
        def _(act):
            act.dma_start(g_s[:, 0:1], g_xattn.partition_broadcast(128)).then_inc(gains_loaded, 16)
            act.dma_start(g_s[:, 1:2], g_ffn.partition_broadcast(128)).then_inc(gains_loaded, 16)
            act.wait_ge(gains_loaded, 32)
            nc.scalar.activation(tanh_s[:, :], g_s[:, :], ACT.Tanh).then_inc(gains_ready, 1)
            act.sem_inc(combT_ready, 1)
            act.sem_inc(yT_ready, 1)

            def front_work(step, b, p):
                if step == "tr1":
                    act.wait_ge(tr1_done, b + 1)
                    nc.scalar.copy(xnT[:, :], misc[:, 0:S]).then_inc(xnT_ready, 1)
                if step in ("q", "k"):
                    done, dst, bias, high = ((q_done, q_s, bq_s, q_high) if step == "q" else
                                             (k_done, k_h, bk_s, k_high))
                    act.wait_ge(done, b + 1)
                    for g in range(G):
                        ins = nc.scalar.activation(dst[:, p, g, :], misc[:, g * S:(g + 1) * S], ACT.Identity,
                                                   bias=bias[:, g:g + 1])
                    ins.then_inc(high, 1)

            def tail_work(step, b, p):
                if step == "tr2":
                    act.wait_ge(tr2_done, b + 1)
                    nc.scalar.copy(x2_h[:, p * S:(p + 1) * S], misc[:, 0:S]).then_inc(x2_high, 1)
                if step == "route":
                    act.wait_ge(logits_ready, b + 1)
                    nc.scalar.activation(prob[:, :, :], logit[:, :, :], ACT.Exp).then_inc(probs_ready, 1)
                if step == "comb":
                    act.wait_ge(combT_done, b + 1)
                    nc.scalar.copy(comb3T[:, p * S:(p + 1) * S], misc[0:3 * EC, 0:S // 2].bitcast(F16))
                    nc.scalar.copy(combT[:, p * S:(p + 1) * S], misc[0:EC, S:2 * S]).then_inc(combT_ready, 1)

            def pt_high_part(b, g, u):
                act.wait_ge(pt_done, len(UNITS) * (G * b + g) + u + 1)
                src, high, _ = pt_parts(g, u)
                nc.scalar.copy(high, src).then_inc(pt_high, 1)

            def attention(b, p, front, tail):
                for step in SCALAR_ORDER:
                    if front:
                        front_work(step, b + 1, 1 - p)
                    if tail:
                        tail_work(step, b - 1, 1 - p)
                    if step[0] == "S":
                        g, j = int(step[1]), int(step[2])
                        n = G * J * b + J * g + j
                        act.wait_ge(max_ready, n + 1)
                        L = 2 * QB * (j + 1)
                        for c in range(2):
                            ins = nc.scalar.activation(p_s[:, g, 2 * j + c, 0:L], sc[j % 4][:, c * S:c * S + L],
                                                       ACT.Exp, bias=negmax[:, g, j, c:c + 1])
                        ins.then_inc(exp_ready, 1)
                        if not tail and g == 1:
                            if j == 0:
                                act.wait_ge(moe_loaded, 16 * N_MOE)
                            for e in range(EX * j // J, EX * (j + 1) // J):
                                nc.scalar.activation(w2_h[:, e, :], w2_s[:, e, :], ACT.Identity,
                                                     scale=mult_s[:, e:e + 1])
                                nc.scalar.copy(w1_h[:, e, :], w1_stage[:, e, :]).then_inc(w_high, 1)
                    if step[0] in "UW":
                        before, g, u = unit(step)
                        if tail or not before:
                            pt_high_part(b - before, g, u)

            def experts(i):
                def high_part_of(e):
                    if e >= LAG:
                        act.wait_ge(down_done, EX * i + e - LAG + 1)
                    act.wait_ge(act_ready, EX * i + e + 2)
                    nc.scalar.copy(act_parts[:, e % LAG, 0, :], act2[:, e % 2, :]).then_inc(act_high, 1)

                act.wait_ge(experts_split, EX)
                for e in range(EX):
                    act.wait_ge(gate_half_done, EX * i + e + 1)
                    nc.scalar.activation(gelu_s[:, e % 2, :], sc[2 * (e % 2) + 1][:, :], ACT.Gelu,
                                         bias=b1g_s[:, e:e + 1]).then_inc(gelu_ready, 1)
                    if e >= 1:
                        high_part_of(e - 1)
                high_part_of(EX - 1)
                act.wait_ge(y_done, i + 1)
                nc.scalar.activation(yT, acc[:, :], ACT.Identity, scale=tanh_s[:, 1:2]).then_inc(yT_ready, 1)

            front_work("tr1", 0, 0)
            act.wait_ge(wq_scaled, 1)
            front_work("q", 0, 0)
            act.wait_ge(attn_loaded, 16 * N_ATTN)
            front_work("k", 0, 0)
            act.wait_ge(probs_cleared, 1)
            attention(0, 0, True, False)
            with act.Fori(0, PAIRS - 1) as i:
                attention(2 * i + 1, 1, True, True)
                attention(2 * i + 2, 0, True, True)
                experts(i)
            attention(B - 1, 1, False, True)
            for u in range(len(UNITS)):
                pt_high_part(B - 1, 1, u)
            for step in ("tr2", "route", "comb"):
                tail_work(step, B - 1, 1)
            experts(PAIRS - 1)

        @block.vector
        def _(dve):
            def own(ins):
                dve.drain()

            dve.sem_inc(act_ready, 1)
            dve.sem_inc(out_ready, 1)
            dve.sem_inc(queries_ready[0], 1)

            def stats_of(b, st, m, v, ready):
                for t in range(TT):
                    ins = nc.vector.bn_stats(st[:, t, :], x_s[:, bass.ds(b, 1), t * 128:(t + 1) * 128])
                own(ins)
                for t in range(TT):
                    ins = nc.vector.bn_aggr(m[:, t, :], st[:, t, :])
                own(ins)
                nc.vector.tensor_scalar(v[:, :], m[:, :, 1], EPS, None, ALU.add).then_inc(ready, 1)

            def low_part(dst, src, bias, high, rows, p, ready):
                for g in range(G):
                    ins = nc.vector.scalar_tensor_tensor(out=dst[rows, p, g, :], in0=src[rows, g * S:(g + 1) * S],
                                                         scalar=bias[rows, g:g + 1], in1=high[rows, p, g, :],
                                                         op0=ALU.add, op1=ALU.subtract)
                ins.then_inc(ready, 1)

            def front_work(step, b, p):
                if step == "ln1a":
                    dve.wait_ge(x0_loaded if isinstance(b, int) and b == 0 else x_loaded, 16)
                    stats_of(b, stats, mv, var, var1_ready)
                if step == "ql":
                    dve.wait_ge(q_high, b + 1)
                    low_part(q_s, misc, bq_s, q_s, slice(64, 128), p, q_ready)
                if step == "kl":
                    dve.wait_ge(k_high, b + 1)
                    low_part(k_l, misc, bk_s, k_h, slice(0, 64), p, k_ready)
                if step[:5] == "heads":
                    dve.wait_ge(q_ready, b + 1)
                    head_block(nc.vector, p, int(step[5]))
                if step == "v":
                    dve.wait_ge(v_done, b + 1)
                    own(nc.vector.tensor_tensor(v_f[:, :].rearrange("p (t f) -> p t f", t=TT),
                                                misc[:, 0:S].rearrange("p (t f) -> p t f", t=TT),
                                                bv_s[:, :].unsqueeze(1).broadcast_to((128, TT, D)), ALU.add))
                    vf = v_f[:, :].rearrange("p (n d) -> p n d", d=DH)
                    vs = v_s[:, p, :, :, :].rearrange("p t h d -> p (t h) d")
                    own(nc.vector.tensor_copy(vs[:, :, 0:DH], vf))
                    nc.vector.tensor_tensor(vs[:, :, DH:2 * DH], vf, vs[:, :, 0:DH], ALU.subtract)\
                        .then_inc(v_ready, 1)

            def tail_work(step, b, p):
                if step == "x2l":
                    dve.wait_ge(x2_high, b + 1)
                    cols = slice(p * S, (p + 1) * S)
                    nc.vector.tensor_tensor(x2_l[:, cols], misc[:, 0:S], x2_h[:, cols],
                                            ALU.subtract).then_inc(x2_ready, 1)
                if step == "gate":
                    dve.wait_ge(gate_done, b + 1)
                    lg = misc[:, 0:TT * EC].rearrange("p (t e) -> p t e", t=TT)[:, :, 0:E]
                    own(nc.vector.tensor_reduce(ngate[:, :], lg, AX.X, ALU.max, negate=True))
                    nc.vector.tensor_tensor(logit[:, :, :], lg, ngate[:, :].unsqueeze(2).broadcast_to((128, TT, E)),
                                            ALU.add).then_inc(logits_ready, 1)
                if step == "route":
                    dve.wait_ge(probs_ready, b + 1)
                    own(nc.vector.tensor_reduce(psum_[:, :], prob[:, :, :], AX.X, ALU.add))
                    own(nc.vector.reciprocal(ngate[:, :], psum_[:, :]))
                    own(nc.vector.tensor_tensor(padded[:, :, 0:E], prob[:, :, :],
                                                ngate[:, :].unsqueeze(2).broadcast_to((128, TT, E)), ALU.mult))
                    for t in range(TT):
                        ins = nc.vector.max(top[:, t, :], padded[:, t, :])
                    own(ins)
                    for t in range(TT):
                        ins = nc.vector.match_replace(rest[:, t, :], top[:, t, :], padded[:, t, :], 0.0)
                    own(ins)
                    nc.vector.tensor_tensor(comb[:, :, 0:E], padded[:, :, 0:E], rest[:, :, 0:E], ALU.subtract)
                    own(nc.vector.tensor_reduce(psum_[:, :], top[:, :, PADS:8], AX.X, ALU.add))
                    own(nc.vector.tensor_scalar(psum_[:, :], psum_[:, :], TOP_EPS, None, ALU.add))
                    own(nc.vector.reciprocal(ngate[:, :], psum_[:, :]))
                    own(nc.vector.tensor_tensor(comb[:, :, 0:E], comb[:, :, 0:E],
                                                ngate[:, :].unsqueeze(2).broadcast_to((128, TT, E)), ALU.mult))
                    own(nc.vector.tensor_copy(comb3[:, :, 0:EC], comb[:, :, :]))
                    own(nc.vector.tensor_tensor(comb_r[:, :, :], comb[:, :, :], comb3[:, :, 0:EC], ALU.subtract))
                    own(nc.vector.tensor_copy(comb3[:, :, EC:2 * EC], comb_r[:, :, :]))
                    nc.vector.tensor_tensor(comb3[:, :, 2 * EC:], comb_r[:, :, :], comb3[:, :, EC:2 * EC],
                                            ALU.subtract).then_inc(comb_ready, 1)

            def normalise_heads(b, g):
                dve.wait_ge(pv_done, G * b + g + 1)
                pv = acc[:, 0:TT * HG * (2 * DH + 1)].rearrange("p (n d) -> p n d", d=2 * DH + 1)
                nc.vector.reciprocal(rden[:, :], pv[:, :, 2 * DH])
                own(nc.vector.tensor_reduce(pv_s[:, :, :],
                                            pv[:, :, 0:2 * DH].rearrange("p n (c d) -> p n d c", c=2), AX.X,
                                            ALU.add))
                nc.vector.tensor_tensor(attn[:, :, HG * g:HG * (g + 1), :],
                                        pv_s[:, :, :].rearrange("p (t h) d -> p t h d", t=TT),
                                        rden[:, :].rearrange("p (t h) -> p t h", t=TT).unsqueeze(3)
                                        .broadcast_to((128, TT, HG, DH)), ALU.mult).then_inc(pv_read, 1)
                if g == G - 1:
                    dve.drain()
                    xb = x_s[:, bass.ds(b, 1), :]
                    own(nc.vector.scalar_tensor_tensor(
                        out=xb, in0=attn[:, :, :, :].rearrange("p t h d -> p (t h d)").unsqueeze(1),
                        scalar=tanh_s[:, 0:1], in1=xb, op0=ALU.mult, op1=ALU.add))
                    stats_of(b, stats2, mv2, var2, var2_ready)

            def pt_low_part(b, g, u):
                dve.wait_ge(pt_high, len(UNITS) * (G * b + g) + u + 1)
                src, high, low = pt_parts(g, u)
                nc.vector.tensor_tensor(low, src, high, ALU.subtract).then_inc(pt_ready, 1)

            def maximum(b, n):
                g, j = n // J, n % J
                dve.wait_ge(scores_done, G * J * b + n + 1)
                pair = sc[j % 4][:, :].rearrange("p (c t) -> p c t", c=2)[:, :, 0:2 * QB * (j + 1)]
                nc.vector.tensor_reduce(negmax[:, g, j, :], pair, AX.X, ALU.max,
                                        negate=True).then_inc(max_ready, 1)

            def attention(b, p, front, tail, ahead=False, next_ahead=False):
                if not ahead:
                    maximum(b, 0)
                for step in VECTOR_ORDER:
                    if front:
                        front_work(step, b + 1, 1 - p)
                    if tail:
                        tail_work(step, b - 1, 1 - p)
                    if step[0] == "S":
                        n = J * int(step[1]) + int(step[2]) + 1
                        if n < G * J:
                            maximum(b, n)
                        elif next_ahead:
                            maximum(b + 1, 0)
                        if not tail and step[1] == "1":
                            j = int(step[2])
                            for e in range(EX * j // J, EX * (j + 1) // J):
                                dve.wait_ge(w_high, e + 1)
                                nc.vector.tensor_tensor(w1_l[:, e, :], w1_stage[:, e, :], w1_h[:, e, :],
                                                        ALU.subtract)
                                nc.vector.scalar_tensor_tensor(out=w2_l[:, e, :], in0=w2_s[:, e, :],
                                                               scalar=mult_s[:, e:e + 1], in1=w2_h[:, e, :],
                                                               op0=ALU.mult, op1=ALU.subtract)\
                                    .then_inc(experts_split, 1)
                    if step[0] in "UW":
                        before, g, u = unit(step)
                        if tail or not before:
                            pt_low_part(b - before, g, u)
                    if step == "N0":
                        normalise_heads(b, 0)
                    if step == "NW" and tail:
                        normalise_heads(b - 1, 1)

            def experts(i, more=True):
                dve.wait_ge(experts_split, EX)
                for e in range(EX):
                    dve.wait_ge(gelu_ready, EX * i + e + 1)
                    dve.wait_ge(up_half_done, EX * i + e + 1)
                    if e >= 2:
                        dve.wait_ge(act_split, EX * i + e - 1)
                    ins = nc.vector.scalar_tensor_tensor(out=act2[:, e % 2, :], in0=sc[2 * (e % 2)][:, :],
                                                         scalar=b1x_s[:, e:e + 1], in1=gelu_s[:, e % 2, :],
                                                         op0=ALU.add, op1=ALU.mult)
                    if e < E:
                        own(ins)
                        dve.wait_ge(weights_done, E * i + e + 1)
                        ins = nc.vector.tensor_tensor(act2[:, e % 2, :], act2[:, e % 2, :], tp[e % 2][:, :],
                                                      ALU.mult)
                    ins.then_inc(act_ready, 1)
                if more:
                    maximum(2 * i + 3, 0)
                dve.wait_ge(yback_done, i + 1)
                xp = x_s[:, bass.ds(2 * i, 2), :]
                nc.vector.tensor_tensor(out_s.rearrange("p (b f) -> p b f", b=2),
                                        misc[:, :].rearrange("p (b f) -> p b f", b=2), xp,
                                        ALU.add).then_inc(out_ready, 1)

            front_work("ln1a", 0, 0)
            dve.wait_ge(wq_loaded, 32)
            nc.vector.tensor_scalar(wq_s[:, :, :], wq_s[:, :, :], DH ** -0.5, None, ALU.mult)
            nc.vector.tensor_scalar(bq_s[:, :], bq_s[:, :], DH ** -0.5, None, ALU.mult).then_inc(wq_scaled, 1)
            nc.vector.memset(v_s[:, :, :, :, 2 * DH:], 1.0)
            nc.vector.memset(padded[:, :, E:], PAD_VALUE)
            nc.vector.memset(comb[:, :, E:], 1.0)
            dve.wait_ge(wq_scaled, 1)
            front_work("ql", 0, 0)
            dve.wait_ge(attn_loaded, 16 * N_ATTN)
            nc.vector.tensor_copy(causal_s[:, :, :], causal_f[:, :, :])
            own(nc.vector.tensor_copy(erw_h[:, :], erw_s[:, :]))
            nc.vector.tensor_tensor(erw_l[:, :], erw_s[:, :], erw_h[:, :], ALU.subtract).then_inc(consts_ready, 1)
            for step in ("kl", "v", "heads0", "heads1"):
                front_work(step, 0, 0)
            dve.wait_ge(q_spread[0][0], 16)
            for part in range(2):
                ins = nc.vector.tensor_tensor(
                    q_over_queries[:, 0, 0, part, :, :].rearrange("p k (h i) -> p k h i", h=HG),
                    q_spread_s[:, HG * part:HG * (part + 1), :].rearrange("p h (k i) -> p k h i", i=QB),
                    qm_s[:, :].unsqueeze(1).unsqueeze(1).broadcast_to((128, NB, HG, QB)), ALU.mult)
            ins.then_inc(queries_ready[0], 1)
            dve.wait_ge(gains_ready, 1)
            attention(0, 0, True, False, next_ahead=True)
            dve.wait_ge(moe_loaded, 16 * N_MOE)
            own(nc.vector.tensor_copy(gate_h[:, :], gate_s[:, :]))
            nc.vector.tensor_tensor(gate_l[:, :], gate_s[:, :], gate_h[:, :], ALU.subtract).then_inc(gate_split, 1)
            with dve.Fori(0, PAIRS - 1) as i:
                attention(2 * i + 1, 1, True, True, ahead=True, next_ahead=True)
                attention(2 * i + 2, 0, True, True, ahead=True)
                dve.wait_ge(out_free, i + 1)
                experts(i)
            attention(B - 1, 1, False, True, ahead=True)
            for u in range(len(UNITS)):
                pt_low_part(B - 1, 1, u)
            normalise_heads(B - 1, 1)
            for step in ("x2l", "gate", "route"):
                tail_work(step, B - 1, 1)
            dve.wait_ge(out_free, PAIRS)
            experts(PAIRS - 1, more=False)

        @block.tensor
        def _(pe):
            mm = nc.tensor.matmul

            def three(out_, stat_h, stat_l, mov_h, mov_l, start=True, stop=True):
                mm(out_, stat_h, mov_h, start=start, stop=False)
                mm(out_, stat_h, mov_l, start=False, stop=False)
                return mm(out_, stat_l, mov_h, start=False, stop=stop)

            def front_work(step, b, p, k):
                if step == "tr1":
                    pe.wait_ge(xn1_ready, b + 1)
                    for t in range(TT):
                        ins = nc.tensor.transpose(misc[:, t * 128:(t + 1) * 128], xn[:, t * 128:(t + 1) * 128],
                                                  id_s[:, :])
                    ins.then_inc(tr1_done, 1)
                if step == "q":
                    pe.wait_ge(xnT_ready, b + 1)
                    for g in range(G):
                        ins = mm(misc[:, g * S:(g + 1) * S], wq_s[:, g, :], xnT[:, :], start=True, stop=True)
                    ins.then_inc(q_done, 1)
                if step == "k":
                    pe.wait_ge(q_ready, b + 1)
                    pe.wait_ge(ctx_loaded[p], 16 * (k + 1))
                    for g in range(G):
                        ins = mm(misc[:, g * S:(g + 1) * S], wk_s[:, g, :], c_s[:, p, :], start=True, stop=True)
                    ins.then_inc(k_done, 1)
                if step == "v":
                    pe.wait_ge(k_ready, b + 1)
                    for t in range(TT):
                        ins = mm(misc[:, t * 128:(t + 1) * 128], c_s[:, p, t * 128:(t + 1) * 128], wv_s[:, :],
                                 start=True, stop=True)
                    ins.then_inc(v_done, 1)

            def tail_work(step, b, p):
                if step == "tr2":
                    pe.wait_ge(xn2_ready, b + 1)
                    for t in range(TT):
                        ins = nc.tensor.transpose(misc[:, t * 128:(t + 1) * 128], xn[:, t * 128:(t + 1) * 128],
                                                  id_s[:, :])
                    ins.then_inc(tr2_done, 1)
                if step == "gate":
                    pe.wait_ge(x2_ready, b + 1)
                    for t in range(TT):
                        cols = slice(p * S + t * 128, p * S + (t + 1) * 128)
                        ins = three(misc[:, t * EC:t * EC + E], x2_h[:, cols], x2_l[:, cols], gate_h[:, :],
                                    gate_l[:, :])
                    ins.then_inc(gate_done, 1)
                if step == "comb":
                    pe.wait_ge(comb_ready, b + 1)
                    for t in range(TT):
                        nc.tensor.transpose(misc[0:EC, S + t * 128:S + (t + 1) * 128], comb[:, t, :], id_s[:, :])
                    for t in range(TT):
                        ins = nc.tensor.transpose(misc[0:3 * EC, t * 64:(t + 1) * 64].bitcast(F16),
                                                  comb3[:, t, :], id16_s[:, :])
                    ins.then_inc(combT_done, 1)

            def scores(p, g, j):
                bank = sc[j % 4]
                L = 2 * QB * (j + 1)
                for c in range(2):
                    n = 2 * j + c
                    u0 = S - 1 - QB * n
                    o = bank[:, c * S:c * S + L]
                    mm(o, q_over_queries[:, p, g, 0, n, :], erw_h[:, u0:u0 + L], start=True, stop=False)
                    mm(o, q_over_queries[:, p, g, 0, n, :], erw_l[:, u0:u0 + L], start=False, stop=False)
                    mm(o, q_over_queries[:, p, g, 1, n, :], erw_h[:, u0:u0 + L], start=False, stop=False)
                    mm(o, q_over_heads[:, p, g, n, :], k_h[:, p, g, 0:L], start=False, stop=False)
                    mm(o, q_over_heads[0:64, p, g, n, :], k_l[:, p, g, 0:L], start=False, stop=False)
                    ins = mm(bank[:, c * S + L - 2 * QB:c * S + L], causal_s[:, c, :], id16_s[0:2 * QB, 0:2 * QB],
                             start=False, stop=True)
                ins.then_inc(scores_done, 1)

            def transposes(b, g, u):
                slot, kt, blk, last = UNITS[u]
                pe.wait_ge(exp_ready, G * J * b + J * g + last + 1)
                if not (isinstance(b, int) and b == 0 and g == 0 and u < 2):
                    pe.wait_ge(pt_ready, len(UNITS) * (G * b + g) + u - 1)
                for n in range(4):
                    ins = nc.tensor.transpose(tp[u % 2][:, n * 128:(n + 1) * 128],
                                              p_s[:, g, blk + n, kt * 128:(kt + 1) * 128], id_s[:, :])
                ins.then_inc(pt_done, 1)

            def values(b, p, g, after_experts=None):
                pe.wait_ge(pt_ready, len(UNITS) * (G * b + g + 1))
                if not (isinstance(b, int) and b == 0 and g == 0):
                    pe.wait_ge(pv_read, G * b + g)
                if after_experts is not None:
                    pe.wait_ge(yT_ready, after_experts + 1)
                for hh in range(HG):
                    for slot, qt, kt in SLOTS:
                        for c in range(2):
                            ins = mm(pv_v[:, qt, hh, :], pt_s[:, slot, c, hh, :], v_s[:, p, kt, HG * g + hh, :],
                                     start=(kt == 0 and c == 0), stop=(kt == qt and c == 1))
                ins.then_inc(pv_done, 1)

            def next_scores(b, p, n):
                g, j = n // J, n % J
                if n == 0:
                    pe.wait_ge(heads_ready[0], b + 1)
                    pe.wait_ge(queries_ready[0], b + 2)
                    pe.wait_ge(k_ready, b + 1)
                if n == J:
                    pe.wait_ge(heads_ready[1], b + 1)
                    pe.wait_ge(queries_ready[1], b + 2)
                if not (isinstance(b, int) and G * J * b + n < 4):
                    pe.wait_ge(exp_ready, G * J * b + n - 3)
                scores(p, g, j)

            def attention(b, p, k, front, tail, after_experts=None, ahead=False, next_ahead=False):
                if not ahead:
                    for n in range(LEAD):
                        next_scores(b, p, n)
                for step in TENSOR_ORDER:
                    if step == ("tr1" if front else "tr2"):
                        pe.wait_ge(v_ready, b + 1)
                        if tail:
                            pe.wait_ge(combT_ready, b)
                        if after_experts is not None:
                            pe.wait_ge(out_ready, after_experts + 1)
                    if tail and front and step == "tr2":
                        pe.wait_ge(v_ready, b + 2)
                    if tail and step == "comb":
                        pe.wait_ge(logits_ready, b)
                    if tail:
                        tail_work(step, b - 1, 1 - p)
                    if front:
                        front_work(step, b + 1, 1 - p, k + p)
                    if step[0] == "S":
                        n = J * int(step[1]) + int(step[2]) + LEAD
                        if n < G * J:
                            next_scores(b, p, n)
                        elif next_ahead:
                            next_scores(b + 1, 1 - p, n - G * J)
                    if step[0] in "UW":
                        before, g, u = unit(step)
                        if tail or not before:
                            transposes(b - before, g, u)
                    if step == "V0":
                        values(b, p, 0)
                    if step == "VW" and tail:
                        values(b - 1, 1 - p, 1, after_experts)

            def experts(i, b_last, groups, more=True):
                def up(e):
                    gate_bank, up_bank = sc[2 * (e % 2) + 1], sc[2 * (e % 2)]
                    if e >= 2:
                        pe.wait_ge(act_ready, EX * i + e)
                    three(gate_bank[:, :], w1_h[:, e, 128:256], w1_l[:, e, 128:256], x2_h[:, :], x2_l[:, :])\
                        .then_inc(gate_half_done, 1)
                    three(up_bank[:, :], w1_h[:, e, 0:128], w1_l[:, e, 0:128], x2_h[:, :], x2_l[:, :])\
                        .then_inc(up_half_done, 1)

                def spread_weights(e):
                    mm(tp[e % 2][:, :], oh_s[:, e, :], comb3T[:, :], start=True, stop=True).then_inc(weights_done, 1)

                def down(e):
                    pe.wait_ge(act_split, EX * i + e + 1)
                    three(acc[:, :], w2_h[:, e, :], w2_l[:, e, :], act_parts[:, e % LAG, 0, :],
                          act_parts[:, e % LAG, 1, :], start=(e == 0), stop=False).then_inc(down_done, 1)

                pe.wait_ge(experts_split, EX)
                pe.wait_ge(x2_ready, 2 * i + 2)
                pe.wait_ge(exp_ready, G * J * (b_last + 1))
                pe.wait_ge(pt_ready, len(UNITS) * groups)
                pe.wait_ge(pv_read, groups)
                up(0)
                up(1)
                if not more:
                    pe.wait_ge(logits_ready, B)
                    tail_work("comb", B - 1, 1)
                pe.wait_ge(combT_ready, 2 * i + 3)
                spread_weights(0)
                spread_weights(1)
                for e in range(2, EX):
                    up(e)
                    if e < E:
                        spread_weights(e)
                    if e >= LAG:
                        down(e - LAG)
                for e in range(EX - LAG, EX):
                    if more and e == EX - LAG + 1:
                        pe.wait_ge(act_ready, EX * i + EX + 1)
                        for n in range(LEAD):
                            next_scores(b_last + 1, 1, n)
                    down(e)
                mm(acc[:, :], b2_s[:, :], combT[:, :], start=False, stop=True).then_inc(y_done, 1)
                pe.wait_ge(yT_ready, i + 2)
                for n in range(2 * TT):
                    ins = nc.tensor.transpose(misc[:, n * 128:(n + 1) * 128], yT[:, n * 128:(n + 1) * 128], id_s[:, :])
                ins.then_inc(yback_done, 1)

            pe.wait_ge(id_loaded, 16)
            front_work("tr1", 0, 0, 0)
            pe.wait_ge(wq_scaled, 1)
            front_work("q", 0, 0, 0)
            pe.wait_ge(attn_loaded, 16 * N_ATTN)
            front_work("k", 0, 0, 0)
            front_work("v", 0, 0, 0)
            pe.wait_ge(consts_ready, 1)
            attention(0, 0, 0, True, False, next_ahead=True)
            pe.wait_ge(moe_loaded, 16 * N_MOE)
            pe.wait_ge(gate_split, 1)
            with pe.Fori(0, PAIRS - 1) as i:
                attention(2 * i + 1, 1, i, True, True, after_experts=i, ahead=True, next_ahead=True)
                attention(2 * i + 2, 0, i + 1, True, True, ahead=True)
                experts(i, 2 * i + 2, G * (2 * i + 2) + 1)
            attention(B - 1, 1, PAIRS - 1, False, True, after_experts=PAIRS - 1, ahead=True)
            for u in range(len(UNITS)):
                transposes(B - 1, 1, u)
            values(B - 1, 1, 1)
            pe.wait_ge(combT_ready, B)
            tail_work("tr2", B - 1, 1)
            tail_work("gate", B - 1, 1)
            experts(PAIRS - 1, B - 1, G * B, more=False)


_ARGS = ["x", "ctxT", "g_xattn", "g_ffn", "wqT", "bq", "wkT", "bk", "wvT", "bv", "erw", "gateT", "w1T", "b1x",
         "b1g", "mult", "w2T", "b2", "identity", "identity16", "head_mask", "query_mask", "causal", "onehot"]


def kernel(**inputs):
    import numpy as np
    import concourse.bacc as bacc
    from concourse.bass_utils import run_bass_kernel_spmd as run

    a = {k: np.asarray(v) for k, v in inputs.items()}
    f32 = np.float32
    er = a["L0_xattn_Er"]
    erw = np.zeros((QB, DH, UW), f32)
    for i in range(QB):
        erw[i, :, i:i + S] = er.T[:, :UW - i]
    sf1, sf2 = a["L0_ffn_s_fc1_w"], a["L0_ffn_s_fc2_w"]
    sb1, sm = a["L0_ffn_s_fc1_b"], a["L0_ffn_s_geglu_mult"]
    s_w1 = np.stack([np.concatenate([sf1[n * 128:(n + 1) * 128], sf1[256 + n * 128:256 + (n + 1) * 128]])
                     for n in range(2)])
    s_b1 = np.stack([np.concatenate([sb1[n * 128:(n + 1) * 128], sb1[256 + n * 128:256 + (n + 1) * 128]])
                     for n in range(2)])
    w1 = np.concatenate([a["L0_ffn_fc1_w"], s_w1])
    b1 = np.concatenate([a["L0_ffn_fc1_b"], s_b1])
    w2 = np.concatenate([a["L0_ffn_fc2_w"], sf2[:, 0:128][None], sf2[:, 128:256][None]])
    mult = np.concatenate([a["L0_ffn_geglu_mult"], sm.reshape(2, 128)])
    head_mask = np.zeros((128, HG, QB), np.float16)
    query_mask = np.zeros((128, QB), np.float16)
    causal = np.zeros((2 * QB, 2, 128), f32)
    onehot = np.zeros((3 * EC, E, 128), np.float16)
    for r in range(128):
        head_mask[r, r // DH % HG] = 1
        query_mask[r, r // DH] = 1
        for c in range(2):
            causal[r % QB + QB * c + 1:, c, r] = MASKED
    twice = lambda w: np.stack([np.concatenate([w[64 * g:64 * g + 64]] * 2) for g in range(G)])
    for e in range(E):
        onehot[e::EC, e, :] = 1
    arrays = {
        "x": a["x"], "ctxT": a["ctx_1024"].reshape(B * S, D).T, "g_xattn": a["g_xattn"], "g_ffn": a["g_ffn"],
        "wqT": twice(a["L0_xattn_Wq"]).transpose(2, 0, 1), "bq": twice(a["L0_xattn_bq"]).T,
        "wkT": twice(a["L0_xattn_Wk"]).transpose(2, 0, 1),
        "bk": twice(a["L0_xattn_bk"]).T, "wvT": a["L0_xattn_Wv"].T, "bv": a["L0_xattn_bv"],
        "erw": erw.reshape(QB * DH, UW), "gateT": a["L0_ffn_gate_w"].T, "w1T": w1.transpose(2, 0, 1),
        "b1x": b1[:, 0:128].T, "b1g": b1[:, 128:256].T, "mult": mult.T, "w2T": w2.transpose(2, 0, 1),
        "b2": np.concatenate([a["L0_ffn_fc2_b"], a["L0_ffn_s_fc2_b"][None]]),
        "identity": np.eye(128, dtype=f32), "identity16": np.eye(128, dtype=np.float16),
        "head_mask": head_mask.reshape(128, 128), "query_mask": query_mask, "causal": causal, "onehot": onehot,
    }
    arrays = {f"in_{k}": np.ascontiguousarray(v) for k, v in arrays.items()}
    nc = bacc.Bacc("TRN2", target_bir_lowering=False, num_devices=1)
    args = [nc.dram_tensor(f"in_{k}", arrays[f"in_{k}"].shape, mybir.dt.from_np(arrays[f"in_{k}"].dtype),
                           kind="ExternalInput").ap() for k in _ARGS]
    out = nc.dram_tensor("out", (B, S, D), F32, kind="ExternalOutput").ap()
    flamingo_block(nc, *args, out)
    return run(nc, [arrays], core_ids=[0]).results[0]["out"]
```
